# Optimizing a Trainium2 kernel written in Bass

```python
import numpy as np
import jax
import jax.numpy as jnp

def _softmax(x, axis=-1):
    return jax.nn.softmax(x, axis=axis)

def _gelu(x):
    return jax.nn.gelu(x, approximate=True)

def _silu(x):
    return jax.nn.silu(x)

def _sigmoid(x):
    return jax.nn.sigmoid(x)

def _layernorm(x, axis=-1, eps=1e-05):
    m = jnp.mean(x, axis=axis, keepdims=True)
    v = jnp.var(x, axis=axis, keepdims=True)
    return (x - m) / jnp.sqrt(v + eps)

def _scatter_add(tgt, idx, src, axis=0):
    return tgt.at[idx].add(src)

def _segment_sum(src, seg, n):
    return jax.ops.segment_sum(src, seg, n)
kernel_name = 'mk_flamingo_gated_d1_seqx_r8_94f6c5'

def setup_inputs(seed: int=0):
    np.random.seed(seed)
    _w = jnp.asarray

    def _rec_inputs():
        import jax
        import jax.numpy as jnp
        _rk = jax.random.key(seed)
        x = -0.0003929 + 0.9999 * jax.random.normal(jax.random.fold_in(_rk, 1), (32, 64, 128), jnp.float32)
        _lenS = 64 - jax.random.randint(jax.random.fold_in(_rk, 7), (32,), 0, max(1, 64 // 4) + 1, jnp.int32)
        _lenS2 = 64 - jax.random.randint(jax.random.fold_in(_rk, 8), (32,), 0, max(1, 64 // 4) + 1, jnp.int32)
        _ctx_512P = jax.random.normal(jax.random.fold_in(_rk, 11), (32, 16, 64), jnp.float32)
        _ctx_512c = jax.random.dirichlet(jax.random.fold_in(_rk, 511), 0.3 * jnp.ones((16,), jnp.float32), (32, 64))
        _ctx_512t = jnp.einsum('bsk,bkd->bsd', _ctx_512c, _ctx_512P)
        _ctx_512t = _ctx_512t * jax.lax.rsqrt(jnp.mean(jnp.square(_ctx_512t)) + 1e-12) * 0.953939
        ctx_512 = -1.39393e-06 + 0.999914 * (_ctx_512t + 0.3 * jax.random.normal(jax.random.fold_in(_rk, 611), (32, 64, 64), jnp.float32))
        _g = jax.random.normal(jax.random.fold_in(_rk, 9001), (2, 1), jnp.float32)
        _g = jnp.sign(_g) * jnp.maximum(jnp.abs(_g), 1.0) + (_g == 0) * 1.0
        g_xattn = _g[0]
        g_ffn = _g[1]
        return (x, ctx_512, g_xattn, g_ffn)
    x, ctx_512, g_xattn, g_ffn = _rec_inputs()

    def _L0_xattn_setup():
        import jax, jax.numpy as jnp
        import numpy as np
        HEADS = 16
        D_MODEL = 128
        IMG_MODEL = 64
        D_K = D_MODEL // HEADS
        key = jax.random.key(seed)
        ks = jax.random.split(key, 12)
        B, LQ, LKV = (8, 256, 128)
        s_dm = 1.0 / np.sqrt(D_MODEL)
        s_im = 1.0 / np.sqrt(IMG_MODEL)
        return {'q': jax.random.normal(ks[0], (B, LQ, D_MODEL), jnp.float32), 'k': jax.random.normal(ks[1], (B, LKV, IMG_MODEL), jnp.float32), 'v': jax.random.normal(ks[2], (B, LKV, IMG_MODEL), jnp.float32), 'Wq': jax.random.normal(ks[3], (D_MODEL, D_MODEL), jnp.float32) * s_dm, 'bq': jnp.zeros((D_MODEL,), jnp.float32), 'Wk': jax.random.normal(ks[4], (IMG_MODEL, D_MODEL), jnp.float32) * s_im, 'bk': jnp.zeros((D_MODEL,), jnp.float32), 'Wv': jax.random.normal(ks[5], (IMG_MODEL, D_MODEL), jnp.float32) * s_im, 'bv': jnp.zeros((D_MODEL,), jnp.float32), 'Wo': jax.random.normal(ks[6], (D_MODEL, D_MODEL), jnp.float32) * s_dm, 'bo': jnp.zeros((D_MODEL,), jnp.float32)}
    _L0_xattn_all = _L0_xattn_setup()
    _L0_xattn_in = {k: v for k, v in _L0_xattn_all.items() if k in ('Wq', 'bq', 'Wk', 'bk', 'Wv', 'bv', 'Wo', 'bo')}
    del _L0_xattn_all

    def _L0_ffn_setup():
        import jax, jax.numpy as jnp
        import numpy as np
        DIM = 128
        N_EXPERTS = 8
        TOPK = 2
        CAPACITY_FACTOR = 1.25
        B, S = (2, 256)

        def _moe(x, Wr, W1, b1, W2, b2):
            Bsz, Sl, D = x.shape
            E = Wr.shape[1]
            T = Bsz * Sl
            capacity = max(1, int(T * CAPACITY_FACTOR / E))
            xt = x.reshape(T, D)
            probs_full = jax.nn.softmax(xt @ Wr, axis=-1)
            topv, topi = jax.lax.top_k(probs_full, TOPK)
            topv = topv / jnp.sum(topv, axis=-1, keepdims=True)
            onehot = jax.nn.one_hot(topi, E, dtype=x.dtype)
            rank = jnp.cumsum(onehot, axis=0)
            keep = (rank <= capacity).astype(x.dtype) * onehot
            w = jnp.einsum('tk,tke->te', topv, keep)
            h = jax.nn.gelu(jnp.einsum('td,edf->etf', xt, W1) + b1[:, None, :], approximate=False)
            y = jnp.einsum('etf,efd->etd', h, W2) + b2[:, None, :]
            out = jnp.einsum('te,etd->td', w, y)
            return out.reshape(Bsz, Sl, D)
        key = jax.random.key(seed)
        ks = jax.random.split(key, 6)
        D, E, F = (DIM, N_EXPERTS, 4 * DIM)
        x = jax.random.normal(ks[0], (B, S, D), dtype=jnp.float32)
        Wr = jax.random.normal(ks[1], (D, E), dtype=jnp.float32) * (1.0 / np.sqrt(D))
        W1 = jax.random.normal(ks[2], (E, D, F), dtype=jnp.float32) * (1.0 / np.sqrt(D))
        b1 = jnp.zeros((E, F), dtype=jnp.float32)
        W2 = jax.random.normal(ks[3], (E, F, D), dtype=jnp.float32) * (1.0 / np.sqrt(F))
        b2 = jnp.zeros((E, D), dtype=jnp.float32)
        return {'x': x, 'Wr': Wr, 'W1': W1, 'b1': b1, 'W2': W2, 'b2': b2}
    _L0_ffn_all = _L0_ffn_setup()
    _L0_ffn_in = {k: v for k, v in _L0_ffn_all.items() if k in ('Wr', 'W1', 'b1', 'W2', 'b2')}
    del _L0_ffn_all
    return {'x': x, 'ctx_512': ctx_512, 'g_xattn': g_xattn, 'g_ffn': g_ffn, 'L0_xattn_Wq': _L0_xattn_in['Wq'], 'L0_xattn_bq': _L0_xattn_in['bq'], 'L0_xattn_Wk': _L0_xattn_in['Wk'], 'L0_xattn_bk': _L0_xattn_in['bk'], 'L0_xattn_Wv': _L0_xattn_in['Wv'], 'L0_xattn_bv': _L0_xattn_in['bv'], 'L0_xattn_Wo': _L0_xattn_in['Wo'], 'L0_xattn_bo': _L0_xattn_in['bo'], 'L0_ffn_Wr': _L0_ffn_in['Wr'], 'L0_ffn_W1': _L0_ffn_in['W1'], 'L0_ffn_b1': _L0_ffn_in['b1'], 'L0_ffn_W2': _L0_ffn_in['W2'], 'L0_ffn_b2': _L0_ffn_in['b2']}

def reference(x, ctx_512, g_xattn, g_ffn, L0_xattn_Wq, L0_xattn_bq, L0_xattn_Wk, L0_xattn_bk, L0_xattn_Wv, L0_xattn_bv, L0_xattn_Wo, L0_xattn_bo, L0_ffn_Wr, L0_ffn_W1, L0_ffn_b1, L0_ffn_W2, L0_ffn_b2):
    import jax
    import jax.numpy as jnp

    def _L0_xattn_ref(q, k, v, Wq, bq, Wk, bk, Wv, bv, Wo, bo):
        import jax, jax.numpy as jnp
        import numpy as np
        HEADS = 16
        D_MODEL = 128
        IMG_MODEL = 64
        D_K = D_MODEL // HEADS
        B, LQ, _ = q.shape
        LKV = k.shape[1]
        qh = (q @ Wq + bq).reshape(B, LQ, HEADS, D_K).transpose(0, 2, 1, 3)
        kh = (k @ Wk + bk).reshape(B, LKV, HEADS, D_K).transpose(0, 2, 1, 3)
        vh = (v @ Wv + bv).reshape(B, LKV, HEADS, D_K).transpose(0, 2, 1, 3)
        scale = 1.0 / np.sqrt(D_K)
        scores = jnp.einsum('bhqd,bhkd->bhqk', qh, kh) * scale
        attn = jax.nn.softmax(scores, axis=-1)
        out = jnp.einsum('bhqk,bhkd->bhqd', attn, vh)
        concat = out.transpose(0, 2, 1, 3).reshape(B, LQ, D_MODEL)
        return concat @ Wo + bo

    def _L0_ffn_ref(x, Wr, W1, b1, W2, b2):
        import jax, jax.numpy as jnp
        import numpy as np
        DIM = 128
        N_EXPERTS = 8
        TOPK = 2
        CAPACITY_FACTOR = 1.25
        B, S = (2, 256)

        def _moe(x, Wr, W1, b1, W2, b2):
            Bsz, Sl, D = x.shape
            E = Wr.shape[1]
            T = Bsz * Sl
            capacity = max(1, int(T * CAPACITY_FACTOR / E))
            xt = x.reshape(T, D)
            probs_full = jax.nn.softmax(xt @ Wr, axis=-1)
            topv, topi = jax.lax.top_k(probs_full, TOPK)
            topv = topv / jnp.sum(topv, axis=-1, keepdims=True)
            onehot = jax.nn.one_hot(topi, E, dtype=x.dtype)
            rank = jnp.cumsum(onehot, axis=0)
            keep = (rank <= capacity).astype(x.dtype) * onehot
            w = jnp.einsum('tk,tke->te', topv, keep)
            h = jax.nn.gelu(jnp.einsum('td,edf->etf', xt, W1) + b1[:, None, :], approximate=False)
            y = jnp.einsum('etf,efd->etd', h, W2) + b2[:, None, :]
            out = jnp.einsum('te,etd->td', w, y)
            return out.reshape(Bsz, Sl, D)
        return _moe(x, Wr, W1, b1, W2, b2)
    x = x + jnp.tanh(g_xattn[0]) * _L0_xattn_ref(_layernorm(x, axis=-1), ctx_512, ctx_512, L0_xattn_Wq, L0_xattn_bq, L0_xattn_Wk, L0_xattn_bk, L0_xattn_Wv, L0_xattn_bv, L0_xattn_Wo, L0_xattn_bo)
    x = x + jnp.tanh(g_ffn[0]) * _L0_ffn_ref(_layernorm(x, axis=-1), L0_ffn_Wr, L0_ffn_W1, L0_ffn_b1, L0_ffn_W2, L0_ffn_b2)
    return x

_drawn_inputs = setup_inputs


def setup_inputs(seed=0):
    import zlib

    import numpy as np

    out = dict(_drawn_inputs(seed))
    spreads = {'L0_xattn_bq': (0.0, 0.1),
     'L0_xattn_bk': (0.0, 0.1),
     'L0_xattn_bv': (0.0, 0.1),
     'L0_xattn_bo': (0.0, 0.1),
     'L0_ffn_b1': (0.0, 0.1),
     'L0_ffn_b2': (0.0, 0.1)}
    factors = {}
    for name, (base, spread) in spreads.items():
        noise = np.random.default_rng([zlib.crc32(name.encode()), seed]).standard_normal(out[name].shape)
        drawn = base * np.exp(spread * noise) if base else spread * noise
        out[name] = jnp.asarray(drawn.astype(out[name].dtype))
    for name, factor in factors.items():
        out[name] = (out[name] * factor).astype(out[name].dtype)
    return out
```

```python
from contextlib import ExitStack

import concourse.bass as bass
from concourse import mybir

F32 = mybir.dt.float32
BF16 = mybir.dt.bfloat16
I32 = mybir.dt.int32
U32 = mybir.dt.uint32
ACT = mybir.ActivationFunctionType
ALU = mybir.AluOpType
AX = mybir.AxisListType

P = 128
HEADS = 16
PAIRS = HEADS // 2
STRIPS = 4
TOP = 2
CAPACITY_FACTOR = 1.25
LN_EPS = 1e-5
OUT_OF_BOUNDS = 1e6
LAST_LAG = 4
WARM_STEPS = LAST_LAG + 2


class Tile:

    def __init__(self, half, ring):
        self.half, self.ring = half, ring
        self.index = half * 2 + ring


def tile_at(step_half, step_ring, lag):
    offset = step_ring - lag
    return Tile(step_half + offset // 2, offset % 2)


def flamingo_block(nc, x, ctx_in, g_xattn, g_ffn, wq, bq, wk, bk, wv, bv, wo, bo, wr, w1, b1, w2, b2,
                   out, slots, picked):
    batches, seq, d_model = x.shape
    d_ctx = ctx_in.shape[2]
    tokens = batches * seq
    tiles = tokens // P
    d_head = d_model // HEADS
    experts, _, d_ff = w1.shape
    f_tiles = d_ff // P
    capacity = max(1, int(tokens * CAPACITY_FACTOR / experts))
    per_expert = TOP * capacity
    slot_tiles = per_expert // P
    first_tiles, first_rest = divmod(capacity, P)
    n_slots = experts * per_expert
    row = d_model + 2 * TOP
    dest_at, weight_at = d_model, d_model + TOP
    v_cols = d_head + 1
    scale = 1.0 / float(d_head) ** 0.5
    assert (d_model, seq, d_head, tiles % 2) == (P, 64, 8, 0) and per_expert % P == 0
    assert slots.shape == (n_slots, row) and picked.shape == (TOP * tokens, d_model)

    x_tiles = x.rearrange("(t b) s d -> (b s) t d", b=2)
    ctx_tiles = ctx_in.rearrange("(t b) s d -> (b s) t d", b=2)
    out_tiles = out.rearrange("(t b) s d -> (b s) t d", b=2)
    slot_rows = slots.rearrange("(e c p) w -> e p c w", p=P, c=slot_tiles)
    picked_rows = picked.rearrange("(k t p) d -> k p t d", k=TOP, p=P)
    wo_split = wo.rearrange("(h j k) n -> j h k n", j=2, k=d_head)

    with ExitStack() as stack:
        def sb(name, shape, dtype=F32):
            return stack.enter_context(nc.sbuf_tensor(name, shape, dtype))

        def sem(name):
            return stack.enter_context(nc.semaphore(name))

        x_sb = sb("x_sb", [P, tiles, d_model])
        ctx_sb = sb("ctx_sb", [P, 2, d_ctx])
        wq_sb = sb("wq_sb", [d_model, d_model])
        wk_sb = sb("wk_sb", [d_ctx, d_model])
        wv_sb = sb("wv_sb", [d_ctx, d_model])
        wo_sb = sb("wo_sb", [PAIRS * d_head, 2, d_model])
        wr_sb = sb("wr_sb", [d_model, experts])
        bias_rows = sb("bias_rows", [experts * f_tiles + 2, P])
        bias_cols = sb("bias_cols", [P, experts * f_tiles + 2])
        bv_all = sb("bv_all", [P, d_model])
        bo_all = sb("bo_all", [P, d_model])
        b2_all = sb("b2_all", [P, experts, d_model])
        gates_in = sb("gates_in", [P, 2])
        gates = sb("gates", [P, 2])
        ident = sb("ident", [P, P])
        tri = sb("tri", [P, P], BF16)
        ones = sb("ones", [P, P], BF16)
        band = sb("band", [P, HEADS])
        head_mask = sb("head_mask", [P, STRIPS])
        expert_ids = sb("expert_ids", [P, experts])
        slot_base = sb("slot_base", [P, TOP, experts])
        over = sb("over", [P, TOP, experts])
        dest_ids = sb("dest_ids", [P, tiles, TOP])
        minus_half = sb("minus_half", [P, 1])
        eps = sb("eps", [P, 1])
        blank = sb("blank", [P, row])

        stats1 = sb("stats1", [P, 6])
        mv1 = sb("mv1", [P, 2, 2])
        var1 = sb("var1", [P, 2])
        rstd1 = sb("rstd1", [P, 2])
        xn1 = sb("xn1", [P, 2, d_model])
        xT = sb("xT", [P, 2, P])
        cT = sb("cT", [d_ctx, 2, P])
        qT = sb("qT", [P, 2, P])
        Qm = sb("Qm", [P, 2, 2, STRIPS, seq])
        Km = sb("Km", [P, 2, 2, STRIPS, seq])
        Vbd = sb("Vbd", [P, 2, PAIRS, 2, 2, v_cols])
        x_bo = sb("x_bo", [P, 2, d_model])
        row_max = sb("row_max", [P, 2, 2, STRIPS])
        probs = sb("probs", [P, 2, PAIRS, 2, seq])
        probsT = sb("probsT", [P, 2, PAIRS, P])
        denom = sb("denom", [P, PAIRS, 2])
        o_norm = sb("o_norm", [P, 2, 2, PAIRS, d_head])
        oT = sb("oT", [PAIRS * d_head, 2, 2, 2 * seq])
        stats2 = sb("stats2", [P, 6])
        mv2 = sb("mv2", [P, 2, 2])
        var2 = sb("var2", [P, 2])
        rstd2 = sb("rstd2", [P, 2])
        rows = sb("rows", [P, 2, row])
        x2T = sb("x2T", [P, 2, P])
        top8 = sb("top8", [P, 2, 8])
        top8_at = sb("top8_at", [P, 8], U32)
        minus_top = sb("minus_top", [P, 2])
        onehot = sb("onehot", [P, 2, TOP, experts], BF16)
        taken = sb("taken", [P, 2, TOP, experts], BF16)
        over_cap = sb("over_cap", [P, TOP, experts])
        based = sb("based", [P, TOP, experts])
        at_any = sb("at_any", [P, TOP, experts])
        at_own = sb("at_own", [P, TOP, experts])
        slot_at = sb("slot_at", [P, 2, TOP], I32)
        top_exp = sb("top_exp", [P, 2, TOP])
        top_sum = sb("top_sum", [P, 2])
        top_inv = sb("top_inv", [P, 1])

        w1_sb = sb("w1_sb", [P, 2, d_ff])
        w2_sb = sb("w2_sb", [P, 2, f_tiles, d_model])
        xg = sb("xg", [P, 2, slot_tiles, row])
        xgT = sb("xgT", [P, 2, per_expert])
        hT = sb("hT", [P, 2, f_tiles, per_expert])
        slot_w = sb("slot_w", [P, 2, slot_tiles])
        slot_dest = sb("slot_dest", [P, 2, slot_tiles], I32)
        y_plus = sb("y_plus", [P, per_expert])
        y_sb = sb("y_sb", [P, 2, slot_tiles, d_model])
        y_back = sb("y_back", [P, TOP, tiles, d_model])

        bank = [stack.enter_context(nc.psum_tensor(f"bank{i}", [P, 512], F32)) for i in range(8)]
        score_bank = bank[0:2]
        turn_bank = bank[2:4]
        o_bank = bank[4]
        act_bank = bank[5]
        qv_bank = bank[6]
        out_bank = bank[7]

        x_loaded = [sem(f"x_loaded{i}") for i in range(3)]
        ctx_loaded = [sem(f"ctx_loaded{i}") for i in range(2)]
        attn_weights = sem("attn_weights")
        small_weights = sem("small_weights")
        blanked = sem("blanked")
        pool_const = sem("pool_const")
        pool_mask = sem("pool_mask")
        dve_const = sem("dve_const")
        bias_turned = sem("bias_turned")
        bias_ready = sem("bias_ready")
        gate_ready = sem("gate_ready")
        gated_bo = sem("gated_bo")
        names = ["stats1", "mv1", "var1", "rstd1", "xn1", "xc_turned", "xc_copied", "q", "v", "k", "q_copied", "v_copied",
                 "k_copied", "q_masked", "x_bo", "scores", "maxima", "shifted", "exps", "probs_turned", "probsT",
                 "pv", "recips", "o_norm", "o_turned", "oT", "projected", "x1", "stats2", "mv2", "var2", "rstd2",
                 "xn2", "x2_turned", "x2T", "logits", "top8", "top8_at", "minus_top", "onehot", "taken", "ranks",
                 "capped", "at_any", "at_own", "slot_at", "top_exp", "top_inv", "weights", "dests"]
        s = {n: sem("s_" + n) for n in names}
        scattered = [sem(f"scattered{i}") for i in range(2)]
        w1_loaded = [sem(f"w1_loaded{i}") for i in range(2)]
        w2_loaded = [sem(f"w2_loaded{i}") for i in range(2)]
        xg_loaded = [sem(f"xg_loaded{i}") for i in range(2)]
        xg_turned = sem("xg_turned")
        xgT_ready = sem("xgT_ready")
        slot_fields = sem("slot_fields")
        up_done = sem("up_done")
        gelu_done = sem("gelu_done")
        down_done = sem("down_done")
        y_biased = sem("y_biased")
        y_ready = sem("y_ready")
        y_stored = [sem(f"y_stored{i}") for i in range(2)]
        y_loaded = [sem(f"y_loaded{i}") for i in range(4)]
        half_sum = sem("half_sum")
        final_sum = sem("final_sum")
        stored = sem("stored")
        dve_waited = sem("dve_waited")
        pe_waited = sem("pe_waited")
        pool_waited = sem("pool_waited")

        block = stack.enter_context(nc.Block())

        def run_steps(eng, step):
            for n in range(WARM_STEPS):
                step(n // 2, n % 2, n)
            with eng.Fori(WARM_STEPS // 2, tiles // 2) as half:
                step(half, 0, None)
                step(half, 1, None)
            for n in range(tiles, tiles + LAST_LAG):
                step(n // 2, n % 2, n)

        def stage(step, lag):
            half, ring, known = step
            if known is not None and not 0 <= known - lag < tiles:
                return None
            return tile_at(half, ring, lag)

        def reused(tile):
            return not isinstance(tile.index, int) or tile.index >= 2

        def after_first(tile):
            return not isinstance(tile.index, int) or tile.index >= 1

        x_pieces = [(0, 2), (2, WARM_STEPS), (WARM_STEPS, tiles)]

        def wait_x(eng, tile):
            for i, (a, b) in enumerate(x_pieces):
                if not isinstance(tile.index, int) or a <= tile.index < b:
                    eng.wait_ge(x_loaded[i], 16)

        @block.sync
        def _(eng):
            def load_x(i):
                a, b = x_pieces[i]
                eng.dma_start(x_sb[:, a:b, :], x_tiles[:, a:b, :]).then_inc(x_loaded[i], 16)

            def load_ctx(t):
                eng.dma_start(ctx_sb[:, t.ring, :], ctx_tiles[:, t.index, :]).then_inc(ctx_loaded[t.ring], 16)

            load_x(0)
            load_ctx(Tile(0, 0))
            eng.dma_start(wq_sb[:, :], wq).then_inc(attn_weights, 16)
            eng.dma_start(wk_sb[:, :], wk).then_inc(attn_weights, 16)
            eng.dma_start(wv_sb[:, :], wv).then_inc(attn_weights, 16)
            load_ctx(Tile(0, 1))
            load_x(1)
            load_x(2)
            for e in range(2):
                eng.dma_start(w1_sb[:, e, :], w1[e]).then_inc(w1_loaded[e], 16)
                eng.dma_start(w2_sb[:, e, :, :], w2[e].rearrange("(f p) d -> p f d", p=P)).then_inc(w2_loaded[e], 16)
            eng.dma_start(b2_all[:, :, :], b2.rearrange("e d -> (e d)").partition_broadcast(P)).then_inc(small_weights, 16)
            with eng.Fori(1, tiles // 2) as half:
                for ring in range(2):
                    t = Tile(half, ring)
                    eng.wait_ge(s["xc_turned"], half * 2 + ring - 1)
                    load_ctx(t)

            for ring in range(2):
                eng.wait_ge(scattered[ring], 16 * TOP * (tiles // 2))
            for e in range(2):
                eng.dma_start(xg[:, e, :, :], slot_rows[e]).then_inc(xg_loaded[e], 16)
            with eng.Fori(1, experts // 2) as half:
                for ring in range(2):
                    e = Tile(half, ring)
                    eng.wait_ge(xg_turned, e.index - 1)
                    eng.wait_ge(slot_fields, e.index - 1)
                    eng.dma_start(xg[:, ring, :, :], slot_rows[e.index]).then_inc(xg_loaded[ring], 16)
                    eng.wait_ge(up_done, f_tiles * (e.index - 1))
                    eng.dma_start(w1_sb[:, ring, :], w1[e.index]).then_inc(w1_loaded[ring], 16)
                    eng.wait_ge(down_done, e.index - 1)
                    eng.dma_start(w2_sb[:, ring, :, :],
                                  w2[e.index].rearrange("(f p) d -> p f d", p=P)).then_inc(w2_loaded[ring], 16)

            for ring in range(2):
                eng.wait_ge(y_stored[ring], 16 * slot_tiles * (experts // 2))
            quarter = tiles // 4
            for c in range(4):
                for k in range(TOP):
                    eng.dma_start(y_back[:, k, c * quarter:(c + 1) * quarter, :],
                                  picked_rows[k, :, c * quarter:(c + 1) * quarter, :]).then_inc(y_loaded[c], 16)
            for c in range(4):
                eng.wait_ge(final_sum, c + 1)
                eng.dma_start(out_tiles[:, c * quarter:(c + 1) * quarter, :],
                              x_sb[:, c * quarter:(c + 1) * quarter, :]).then_inc(stored, 16)
            eng.wait_ge(stored, 64)

        @block.gpsimd
        def _(eng):
            eng.memset(ident[:, :], 0.0).then_inc(pool_const, 1)
            eng.memset(ones[:, :], 1.0).then_inc(pool_const, 1)
            eng.memset(minus_half[:, :], -0.5).then_inc(pool_const, 1)
            eng.memset(eps[:, :], LN_EPS)
            eng.memset(band[:, :], 1.0).then_inc(pool_const, 1)
            eng.wait_ge(pool_const, 4)
            eng.affine_select(out=ident[:, :], in_=ident[:, :], compare_op=ALU.not_equal, fill=1.0, base=0,
                              pattern=[[-1, P]], channel_multiplier=1).then_inc(pool_const, 1)
            eng.affine_select(out=band[:, :], in_=band[:, :], compare_op=ALU.is_ge, fill=0.0, base=0,
                              pattern=[[-d_head, HEADS]], channel_multiplier=1).then_inc(pool_const, 1)
            eng.wait_ge(pool_const, 6)
            eng.affine_select(out=band[:, :], in_=band[:, :], compare_op=ALU.is_ge, fill=0.0, base=d_head - 1,
                              pattern=[[d_head, HEADS]], channel_multiplier=-1).then_inc(pool_const, 1)
            eng.affine_select(out=tri[:, :], in_=ones[:, :], compare_op=ALU.is_ge, fill=0.0, base=0,
                              pattern=[[1, P]], channel_multiplier=-1).then_inc(pool_const, 1)
            eng.iota(expert_ids[:, :], pattern=[[1, experts]], base=0, channel_multiplier=0,
                     allow_small_or_imprecise_dtypes=True).then_inc(pool_const, 1)
            eng.iota(slot_base[:, :, :], pattern=[[capacity, TOP], [per_expert, experts]], base=-1,
                     channel_multiplier=0, allow_small_or_imprecise_dtypes=True).then_inc(pool_const, 1)
            eng.iota(dest_ids[:, :, :], pattern=[[P, tiles], [tokens, TOP]], base=0, channel_multiplier=1,
                     allow_small_or_imprecise_dtypes=True).then_inc(pool_const, 1)
            eng.memset(over[:, :, :], OUT_OF_BOUNDS).then_inc(pool_const, 1)
            eng.memset(taken[:, 0, :, :], 0.0).then_inc(s["taken"], 1)

            def inv_std(t, mv, var, rstd, mv_name, var_name, rstd_name, readers):
                eng.wait_ge(s[mv_name], t.index + 1)
                eng.tensor_tensor(var[:, t.ring:t.ring + 1], mv[:, t.ring, 1:2], eps[:, :],
                                  ALU.add).then_inc(s[var_name], 1)
                eng.wait_ge(s[var_name], t.index + 1)
                if reused(t):
                    eng.wait_ge(s[readers], t.index - 1)
                eng.tensor_tensor(rstd[:, t.ring:t.ring + 1], var[:, t.ring:t.ring + 1], minus_half[:, :],
                                  ALU.pow).then_inc(s[rstd_name], 1)

            def step(half, ring, known):
                at = (half, ring, known)
                t = stage(at, 0)
                if t:
                    inv_std(t, mv1, var1, rstd1, "mv1", "var1", "rstd1", "xn1")
                t = stage(at, 4)
                if t:
                    if reused(t):
                        eng.wait_ge(scattered[t.ring], 16 * TOP * t.half)
                    eng.tensor_copy(rows[:, t.ring, dest_at:dest_at + TOP],
                                    dest_ids[:, t.index, :]).then_inc(s["dests"], 1)
                t = stage(at, 2)
                if t:
                    if known == 2:
                        eng.wait_ge(gated_bo, 1)
                    wait_x(eng, t)
                    if reused(t):
                        eng.wait_ge(s["x1"], t.index - 1)
                    eng.tensor_tensor(x_bo[:, t.ring, :], x_sb[:, t.index, :], bo_all[:, :],
                                      ALU.add).then_inc(s["x_bo"], 1)
                t = stage(at, 0)
                if t:
                    eng.wait_ge(s["q_copied"], t.index + 1)
                    if known == 0:
                        eng.wait_ge(pool_mask, 1)
                    if reused(t):
                        eng.wait_ge(s["scores"], t.index * 2 - 2)
                    for b in range(2):
                        last = eng.tensor_tensor(
                            Qm[:, t.ring, b, :, :],
                            qT[:, t.ring, b * seq:(b + 1) * seq].unsqueeze(1).broadcast_to([P, STRIPS, seq]),
                            head_mask[:, :].unsqueeze(2).broadcast_to([P, STRIPS, seq]), ALU.mult)
                    last.then_inc(s["q_masked"], 1)
                t = stage(at, 4)
                if t:
                    eng.wait_ge(s["onehot"], t.index + 1)
                    eng.wait_ge(s["taken"], t.index + 1)
                    if after_first(t):
                        eng.wait_ge(s["ranks"], t.index)
                    eng.tensor_tensor(taken[:, 1 - t.ring, :, :], taken[:, t.ring, :, :], onehot[:, t.ring, :, :],
                                      ALU.add).then_inc(s["taken"], 1)
                    if known == 4:
                        eng.wait_ge(blanked, 32)
                    eng.wait_ge(s["slot_at"], t.index + 1)
                    eng.wait_ge(s["weights"], t.index + 1)
                    eng.wait_ge(s["dests"], t.index + 1)
                    eng.sem_inc(pool_waited, 1)
                    for k in range(TOP):
                        eng.indirect_dma_start(
                            out=slots[:, :], out_offset=bass.IndirectOffsetOnAxis(ap=slot_at[:, t.ring, k:k + 1], axis=0),
                            in_=rows[:, t.ring, :], in_offset=None, bounds_check=n_slots - 1,
                            oob_is_err=False).then_inc(scattered[t.ring], 16)
                t = stage(at, 3)
                if t:
                    inv_std(t, mv2, var2, rstd2, "mv2", "var2", "rstd2", "xn2")

            run_steps(eng, step)

            def send_rows(e):
                eng.wait_ge(y_ready, e.index + 1)
                eng.wait_ge(slot_fields, e.index + 1)
                eng.sem_inc(pool_waited, 1)
                for c in range(slot_tiles):
                    eng.indirect_dma_start(
                        out=picked[:, :], out_offset=bass.IndirectOffsetOnAxis(ap=slot_dest[:, e.ring, c:c + 1], axis=0),
                        in_=y_sb[:, e.ring, c, :], in_offset=None, bounds_check=TOP * tokens - 1,
                        oob_is_err=False).then_inc(y_stored[e.ring], 16)

            with eng.Fori(0, experts // 2) as half:
                for ring in range(2):
                    send_rows(Tile(half, ring))

        @block.scalar
        def _(eng):
            eng.dma_start(gates_in[:, 0:1], g_xattn.partition_broadcast(P)).then_inc(small_weights, 16)
            eng.dma_start(gates_in[:, 1:2], g_ffn.partition_broadcast(P)).then_inc(small_weights, 16)
            n_b1 = experts * f_tiles
            eng.dma_start(bias_rows[0:n_b1, :], b1.rearrange("e (f p) -> (e f) p", p=P)).then_inc(attn_weights, 16)
            eng.dma_start(bias_rows[n_b1:n_b1 + 1, :], bq.rearrange("(a n) -> a n", a=1)).then_inc(attn_weights, 16)
            eng.dma_start(bias_rows[n_b1 + 1:n_b1 + 2, :], bk.rearrange("(a n) -> a n", a=1)).then_inc(attn_weights, 16)
            eng.dma_start(bv_all[:, :], bv.partition_broadcast(P)).then_inc(small_weights, 16)
            eng.dma_start(bo_all[:, :], bo.partition_broadcast(P)).then_inc(small_weights, 16)
            for j in range(2):
                eng.dma_start(wo_sb[:, j, :], wo_split[j]).then_inc(small_weights, 16)
            eng.dma_start(wr_sb[:, :], wr).then_inc(small_weights, 16)
            eng.wait_ge(dve_const, 3)
            eng.dma_start(slots.rearrange("(n p) w -> p n w", p=P),
                          blank[:, :].unsqueeze(1).broadcast_to([P, n_slots // P, row])).then_inc(blanked, 16)
            eng.dma_start(picked.rearrange("(n p) w -> p n w", p=P),
                          blank[:, 0:d_model].unsqueeze(1).broadcast_to([P, TOP * tokens // P, d_model])).then_inc(blanked, 16)
            eng.wait_ge(small_weights, 16 * 8)
            eng.activation(gates[:, :], gates_in[:, :], ACT.Tanh).then_inc(gate_ready, 1)
            eng.wait_ge(bias_turned, 1)
            eng.activation(bias_cols[:, :], act_bank[:, 0:n_b1 + 2], ACT.Copy).then_inc(bias_ready, 1)
            eng.wait_ge(bias_ready, 1)

            def step(half, ring, known):
                at = (half, ring, known)
                t = stage(at, 4)
                if t:
                    eng.wait_ge(s["x2_turned"], t.index + 1)
                    if reused(t):
                        eng.wait_ge(s["logits"], t.index - 1)
                    eng.activation(x2T[:, t.ring, :], act_bank[:, 0:P], ACT.Copy).then_inc(s["x2T"], 1)
                t = stage(at, 2)
                if t:
                    for h in range(2):
                        eng.wait_ge(s["probs_turned"], t.index * 2 + h + 1)
                        if reused(t):
                            eng.wait_ge(s["pv"], t.index - 1)
                        eng.activation(probsT[:, t.ring, 4 * h:4 * h + 4, :],
                                       turn_bank[h][:, :], ACT.Copy).then_inc(s["probsT"], 1)
                t = stage(at, 0)
                if t:
                    eng.wait_ge(s["xc_turned"], t.index + 1)
                    if reused(t):
                        eng.wait_ge(s["v"], t.index - 1)
                        eng.wait_ge(s["k"], t.index - 1)
                    eng.activation(xT[:, t.ring, :], act_bank[:, 0:P], ACT.Copy)
                    eng.activation(cT[:, t.ring, :], act_bank[0:d_ctx, P:2 * P], ACT.Copy).then_inc(s["xc_copied"], 1)
                t = stage(at, 3)
                if t:
                    eng.wait_ge(s["o_turned"], t.index + 1)
                    if reused(t):
                        eng.wait_ge(s["projected"], t.index - 1)
                    eng.activation(oT[:, t.ring, :, :].rearrange("k j (b q) -> k b j q", b=2),
                                   act_bank[0:PAIRS * d_head, 0:2 * P].rearrange("k (b j q) -> k b j q", b=2, j=2),
                                   ACT.Copy).then_inc(s["oT"], 1)
                t = stage(at, 0)
                if t:
                    eng.wait_ge(s["k"], t.index + 1)
                    if known == 0:
                        eng.wait_ge(dve_const, 3)
                    if reused(t):
                        eng.wait_ge(s["scores"], t.index * 2 - 2)
                    for j in range(STRIPS):
                        r = slice(32 * j, 32 * j + 32)
                        last = eng.activation(Km[r, t.ring, :, j, :],
                                              act_bank[r, 2 * P:3 * P].rearrange("p (b k) -> p b k", b=2),
                                              ACT.Identity, bias=bias_cols[r, n_b1 + 1:n_b1 + 2])
                    last.then_inc(s["k_copied"], 1)
                t = stage(at, 1)
                if t:
                    eng.wait_ge(s["shifted"], t.index * 2 + 2)
                    eng.activation(probs[:, t.ring], probs[:, t.ring], ACT.Exp).then_inc(s["exps"], 1)
                t = stage(at, 4)
                if t:
                    eng.wait_ge(s["minus_top"], t.index + 1)
                    if reused(t):
                        eng.wait_ge(s["weights"], t.index - 1)
                    eng.activation(top_exp[:, t.ring, :], top8[:, t.ring, 0:TOP], ACT.Exp,
                                   bias=minus_top[:, t.ring:t.ring + 1],
                                   accum_out=top_sum[:, t.ring:t.ring + 1]).then_inc(s["top_exp"], 1)

            run_steps(eng, step)

            def gelus(e):
                for f in range(f_tiles):
                    eng.wait_ge(up_done, e.index * f_tiles + f + 1)
                    if reused(e):
                        eng.wait_ge(down_done, e.index - 1)
                    for h in range(2):
                        last = eng.activation(
                            hT[:, e.ring, f, h * capacity:(h + 1) * capacity], bank[2 * (f % 2) + h][:, 0:capacity],
                            ACT.Gelu, bias=bias_cols[:, bass.ds(e.index * f_tiles + f, 1)])
                    last.then_inc(gelu_done, 1)

            gelus(Tile(0, 0))
            gelus(Tile(0, 1))
            with eng.Fori(1, experts // 2) as half:
                for ring in range(2):
                    gelus(Tile(half, ring))

        @block.vector
        def _(eng):
            eng.memset(blank[:, :], 0.0).then_inc(dve_const, 1)
            eng.wait_ge(dve_const, 1)
            eng.memset(blank[:, dest_at:dest_at + TOP], OUT_OF_BOUNDS).then_inc(dve_const, 1)
            eng.memset(Km[:, :, :, :, :], 0.0)
            eng.memset(Vbd[:, :, :, :, :, 0:d_head], 0.0).then_inc(dve_const, 1)
            for b in range(2):
                own = slice(64 * b, 64 * b + 64)
                for c in range(2):
                    last = eng.memset(Vbd[own, :, :, c, :, d_head:v_cols], 1.0 if b == c else 0.0)
            last.then_inc(dve_const, 1)
            eng.wait_ge(pool_const, 12)
            eng.tensor_reduce(head_mask[:, :], band[:, :].rearrange("p (s h) -> p h s", h=STRIPS), AX.X,
                              ALU.add).then_inc(pool_mask, 1)
            eng.wait_ge(dve_const, 4)
            eng.wait_ge(gate_ready, 1)
            eng.tensor_scalar(bo_all[:, :], bo_all[:, :], gates[:, 0:1], None, ALU.mult).then_inc(gated_bo, 1)
            bq_col = bias_cols[:, experts * f_tiles:experts * f_tiles + 1]

            def layer_stats(t, source, stats, mv, stats_name, mv_name, readers):
                if after_first(t):
                    eng.wait_ge(s[mv_name], t.index)
                eng.sem_inc(dve_waited, 1)
                eng.bn_stats(stats[:, :], source).then_inc(s[stats_name], 1)
                eng.wait_ge(s[stats_name], t.index + 1)
                if reused(t):
                    eng.wait_ge(s[readers], t.index - 1)
                eng.sem_inc(dve_waited, 1)
                eng.bn_aggr(mv[:, t.ring, :], stats[:, :]).then_inc(s[mv_name], 1)

            def normalise(t, source, mv, rstd, to, done):
                eng.tensor_scalar(to, source, mv[:, t.ring, 0:1], rstd[:, t.ring:t.ring + 1], ALU.subtract,
                                  ALU.mult).then_inc(s[done], 1)

            def shift_scores(t, b):
                n = t.index * 2 + b
                eng.wait_ge(s["scores"], n + 1)
                if not isinstance(t.index, int) or n >= 2:
                    eng.wait_ge(s["shifted"], n - 1)
                scores = score_bank[b][:, :].rearrange("p (g s k) -> p g s k", g=2, k=seq)
                eng.tensor_reduce(row_max[:, b, :, :], scores, AX.X, ALU.max).then_inc(s["maxima"], 1)
                eng.wait_ge(s["maxima"], n + 1)
                if reused(t):
                    eng.wait_ge(s["probs_turned"], t.index * 2 - 2)
                eng.tensor_tensor(probs[:, t.ring, :, b, :].rearrange("p (s g) k -> p g s k", g=2), scores,
                                  row_max[:, b, :, :].unsqueeze(3).broadcast_to([P, 2, STRIPS, seq]),
                                  ALU.subtract).then_inc(s["shifted"], 1)

            def step(half, ring, known):
                at = (half, ring, known)
                t = stage(at, 0)
                if t:
                    wait_x(eng, t)
                    layer_stats(t, x_sb[:, t.index, :], stats1, mv1, "stats1", "mv1", "xn1")
                t = stage(at, 4)
                if t:
                    eng.wait_ge(s["rstd2"], t.index + 1)
                    if reused(t):
                        eng.wait_ge(scattered[t.ring], 16 * TOP * t.half)
                    normalise(t, x_sb[:, t.index, :], mv2, rstd2, rows[:, t.ring, 0:d_model], "xn2")
                t = stage(at, 1)
                if t:
                    shift_scores(t, 0)
                t = stage(at, 0)
                if t:
                    eng.wait_ge(s["rstd1"], t.index + 1)
                    if reused(t):
                        eng.wait_ge(s["xc_turned"], t.index - 1)
                    normalise(t, x_sb[:, t.index, :], mv1, rstd1, xn1[:, t.ring, :], "xn1")
                t = stage(at, 1)
                if t:
                    eng.wait_ge(s["v"], t.index + 1)
                    if reused(t):
                        eng.wait_ge(s["pv"], t.index - 1)
                    for b in range(2):
                        own = slice(64 * b, 64 * b + 64)
                        last = eng.tensor_tensor(
                            Vbd[own, t.ring, :, b, :, 0:d_head],
                            qv_bank[own, P:2 * P].rearrange("p (h j k) -> p h j k", j=2, k=d_head),
                            bv_all[own, :].rearrange("p (h j k) -> p h j k", j=2, k=d_head), ALU.add)
                    last.then_inc(s["v_copied"], 1)
                t = stage(at, 1)
                if t:
                    shift_scores(t, 1)
                t = stage(at, 4)
                if t:
                    logits = out_bank[:, P:P + experts]
                    eng.wait_ge(s["logits"], t.index + 1)
                    if reused(t):
                        eng.wait_ge(s["top_exp"], t.index - 1)
                    eng.sem_inc(dve_waited, 1)
                    eng.max(top8[:, t.ring, :], logits).then_inc(s["top8"], 1)
                    eng.wait_ge(s["top8"], t.index + 1)
                    if after_first(t):
                        eng.wait_ge(s["onehot"], t.index)
                    eng.sem_inc(dve_waited, 1)
                    eng.max_index(top8_at[:, :], top8[:, t.ring, :], logits).then_inc(s["top8_at"], 1)
                    eng.tensor_scalar(minus_top[:, t.ring:t.ring + 1], top8[:, t.ring, 0:1], -1.0, None,
                                      ALU.mult).then_inc(s["minus_top"], 1)
                    eng.wait_ge(s["top8_at"], t.index + 1)
                    if reused(t):
                        eng.wait_ge(s["taken"], t.index)
                        eng.wait_ge(s["ranks"], t.index - 1)
                    eng.tensor_tensor(onehot[:, t.ring, :, :],
                                      expert_ids[:, :].unsqueeze(1).broadcast_to([P, TOP, experts]),
                                      top8_at[:, 0:TOP].unsqueeze(2).broadcast_to([P, TOP, experts]),
                                      ALU.is_equal).then_inc(s["onehot"], 1)
                t = stage(at, 0)
                if t:
                    if known == 0:
                        eng.wait_ge(bias_ready, 1)
                    eng.wait_ge(s["q"], t.index + 1)
                    if reused(t):
                        eng.wait_ge(s["q_masked"], t.index - 1)
                    eng.tensor_scalar(qT[:, t.ring, :], qv_bank[:, 0:P], bq_col, scale, ALU.add,
                                      ALU.mult).then_inc(s["q_copied"], 1)
                t = stage(at, 4)
                if t:
                    rank = out_bank[:, 144:144 + TOP * experts].rearrange("p (k e) -> p k e", k=TOP)
                    eng.wait_ge(s["ranks"], t.index + 1)
                    if after_first(t):
                        eng.wait_ge(s["at_any"], t.index)
                    eng.scalar_tensor_tensor(out=over_cap[:, :, :], in0=rank, scalar=float(capacity),
                                             in1=over[:, :, :], op0=ALU.is_gt, op1=ALU.mult)
                    eng.tensor_tensor(based[:, :, :], rank, slot_base[:, :, :], ALU.add).then_inc(s["capped"], 1)
                    eng.wait_ge(s["capped"], t.index + 1)
                    if after_first(t):
                        eng.wait_ge(s["at_own"], t.index)
                    eng.tensor_tensor(at_any[:, :, :], over_cap[:, :, :], based[:, :, :],
                                      ALU.add).then_inc(s["at_any"], 1)
                    eng.wait_ge(s["at_any"], t.index + 1)
                    if after_first(t):
                        eng.wait_ge(s["slot_at"], t.index)
                    eng.tensor_tensor(at_own[:, :, :], at_any[:, :, :], onehot[:, t.ring, :, :],
                                      ALU.mult).then_inc(s["at_own"], 1)
                    eng.wait_ge(s["at_own"], t.index + 1)
                    with nc.allow_low_precision(reason="the sum of one whole number and zeros, exact in int32"):
                        eng.tensor_reduce(slot_at[:, t.ring, :], at_own[:, :, :], AX.X,
                                          ALU.add).then_inc(s["slot_at"], 1)
                t = stage(at, 3)
                if t:
                    eng.wait_ge(s["projected"], t.index + 1)
                    eng.wait_ge(s["x_bo"], t.index + 1)
                    eng.scalar_tensor_tensor(out=x_sb[:, t.index, :], in0=out_bank[:, 0:P], scalar=gates[:, 0:1],
                                             in1=x_bo[:, t.ring, :], op0=ALU.mult, op1=ALU.add).then_inc(s["x1"], 1)
                    eng.wait_ge(s["x1"], t.index + 1)
                    layer_stats(t, x_sb[:, t.index, :], stats2, mv2, "stats2", "mv2", "xn2")
                t = stage(at, 4)
                if t:
                    eng.wait_ge(s["top_exp"], t.index + 1)
                    if after_first(t):
                        eng.wait_ge(s["weights"], t.index)
                    eng.reciprocal(top_inv[:, :], top_sum[:, t.ring:t.ring + 1]).then_inc(s["top_inv"], 1)
                    eng.wait_ge(s["top_inv"], t.index + 1)
                    eng.tensor_scalar(rows[:, t.ring, weight_at:weight_at + TOP], top_exp[:, t.ring, :],
                                      top_inv[:, 0:1], gates[:, 1:2], ALU.mult, ALU.mult).then_inc(s["weights"], 1)
                t = stage(at, 2)
                if t:
                    o = o_bank[:, 0:PAIRS * 4 * v_cols].rearrange("p (h b j k) -> p h b j k", b=2, j=2, k=v_cols)
                    eng.wait_ge(s["pv"], t.index + 1)
                    if after_first(t):
                        eng.wait_ge(s["o_norm"], t.index)
                    for j in range(2):
                        own = slice(64 * j, 64 * j + 64)
                        last = eng.reciprocal(denom[own, :, :], o[own, :, :, j, d_head])
                    last.then_inc(s["recips"], 1)
                    eng.wait_ge(s["recips"], t.index + 1)
                    if reused(t):
                        eng.wait_ge(s["o_turned"], t.index - 1)
                    for j in range(2):
                        own = slice(64 * j, 64 * j + 64)
                        last = eng.tensor_tensor(
                            o_norm[own, t.ring, :, :, :].rearrange("p b h k -> p h b k"), o[own, :, :, j, 0:d_head],
                            denom[own, :, :].unsqueeze(3).broadcast_to([64, PAIRS, 2, d_head]), ALU.mult)
                    last.then_inc(s["o_norm"], 1)

            run_steps(eng, step)

            split = min(512, per_expert)

            def turn_in(e):
                eng.wait_ge(xg_turned, e.index + 1)
                if reused(e):
                    eng.wait_ge(up_done, f_tiles * (e.index - 1))
                eng.tensor_copy(xgT[:, e.ring, 0:split], bank[6][:, 0:split])
                eng.tensor_copy(xgT[:, e.ring, split:per_expert], bank[7][:, 0:per_expert - split]).then_inc(xgT_ready, 1)
                eng.wait_ge(xg_loaded[e.ring], 16 * (e.half + 1))
                if reused(e):
                    eng.wait_ge(y_stored[e.ring], 16 * slot_tiles * e.half)
                    eng.wait_ge(y_ready, e.index - 1)
                for field, to in ((weight_at, slot_w), (dest_at, slot_dest)):
                    eng.tensor_copy(to[:, e.ring, 0:first_tiles], xg[:, e.ring, 0:first_tiles, field])
                    for part, k in ((slice(0, first_rest), 0), (slice(first_rest, P), 1)):
                        eng.tensor_copy(to[part, e.ring, first_tiles:first_tiles + 1],
                                        xg[part, e.ring, first_tiles:first_tiles + 1, field + k])
                    last = eng.tensor_copy(to[:, e.ring, first_tiles + 1:slot_tiles],
                                           xg[:, e.ring, first_tiles + 1:slot_tiles, field + 1])
                last.then_inc(slot_fields, 1)

            def turn_out(e):
                eng.wait_ge(down_done, e.index + 1)
                if after_first(e):
                    eng.wait_ge(y_ready, e.index)
                full = split // P
                eng.tensor_tensor(y_plus[:, 0:split].rearrange("p (c d) -> p c d", d=d_model),
                                  bank[4][:, 0:split].rearrange("p (c d) -> p c d", d=d_model),
                                  b2_all[:, bass.ds(e.index, 1), :].broadcast_to([P, full, d_model]), ALU.add)
                eng.tensor_tensor(y_plus[:, split:per_expert].rearrange("p (c d) -> p c d", d=d_model),
                                  bank[5][:, 0:per_expert - split].rearrange("p (c d) -> p c d", d=d_model),
                                  b2_all[:, bass.ds(e.index, 1), :].broadcast_to([P, slot_tiles - full, d_model]),
                                  ALU.add).then_inc(y_biased, 1)
                eng.wait_ge(y_biased, e.index + 1)
                eng.wait_ge(slot_fields, e.index + 1)
                if reused(e):
                    eng.wait_ge(y_stored[e.ring], 16 * slot_tiles * e.half)
                eng.tensor_tensor(y_sb[:, e.ring, :, :], y_plus[:, :].rearrange("p (c d) -> p c d", d=d_model),
                                  slot_w[:, e.ring, :].unsqueeze(2).broadcast_to([P, slot_tiles, d_model]),
                                  ALU.mult).then_inc(y_ready, 1)

            turn_in(Tile(0, 0))
            turn_in(Tile(0, 1))
            turn_out(Tile(0, 0))
            turn_in(Tile(1, 0))
            turn_out(Tile(0, 1))
            with eng.Fori(1, experts // 2 - 1) as half:
                turn_in(Tile(half, 1))
                turn_out(Tile(half, 0))
                turn_in(Tile(half + 1, 0))
                turn_out(Tile(half, 1))
            end = experts // 2 - 1
            turn_in(Tile(end, 1))
            turn_out(Tile(end, 0))
            turn_out(Tile(end, 1))

            quarter = tiles // 4
            for c in range(4):
                part = slice(c * quarter, (c + 1) * quarter)
                eng.wait_ge(y_loaded[c], 16 * TOP)
                for k in range(TOP):
                    if k:
                        eng.wait_ge(half_sum, c + 1)
                    eng.tensor_tensor(x_sb[:, part, :], x_sb[:, part, :], y_back[:, k, part, :],
                                      ALU.add).then_inc(final_sum if k else half_sum, 1)

        @block.tensor
        def _(eng):
            eng.wait_ge(pool_const, 12)
            eng.wait_ge(attn_weights, 16 * 6)
            n_rows = experts * f_tiles + 2
            eng.transpose(act_bank[:, 0:n_rows], bias_rows[:, :], ident[0:n_rows, 0:n_rows]).then_inc(bias_turned, 1)

            def step(half, ring, known):
                at = (half, ring, known)
                t = stage(at, 1)
                if t:
                    eng.wait_ge(s["q_masked"], t.index + 1)
                    eng.wait_ge(s["k_copied"], t.index + 1)
                    for b in range(2):
                        if after_first(t):
                            eng.wait_ge(s["shifted"], t.index * 2 - 1 + b)
                        for g in range(2):
                            mm = eng.matmul(score_bank[b][:, 256 * g:256 * g + 256],
                                            Qm[:, t.ring, b, 2 * g:2 * g + 2, :].rearrange("p j q -> p (j q)"),
                                            Km[:, t.ring, b, :, :].rearrange("p s k -> p (s k)"),
                                            start=True, stop=True)
                        mm.then_inc(s["scores"], 1)
                t = stage(at, 1)
                if t:
                    eng.matmul(qv_bank[:, P:2 * P], cT[:, t.ring, :], wv_sb[:, :], start=True,
                               stop=True).then_inc(s["v"], 1)
                t = stage(at, 4)
                if t:
                    eng.wait_ge(s["xn2"], t.index + 1)
                    eng.wait_ge(s["k_copied"], t.index + 4 if known is None else min(known, tiles))
                    eng.wait_ge(s["oT"], t.index + 1)
                    eng.transpose(act_bank[:, 0:P], rows[:, t.ring, 0:d_model], ident[:, :]).then_inc(s["x2_turned"], 1)
                t = stage(at, 2)
                if t:
                    eng.wait_ge(s["exps"], t.index + 1)
                    for h in range(2):
                        if after_first(t):
                            eng.wait_ge(s["probsT"], t.index * 2 - 1 + h)
                        for i in range(4):
                            p = 4 * h + i
                            mm = eng.transpose(turn_bank[h][:, i * P:(i + 1) * P],
                                               probs[:, t.ring, p, :, :].rearrange("p b k -> p (b k)"), ident[:, :])
                        mm.then_inc(s["probs_turned"], 1)
                t = stage(at, 0)
                if t:
                    eng.wait_ge(s["xn1"], t.index + 1)
                    eng.wait_ge(ctx_loaded[t.ring], 16 * (t.half + 1))
                    if known == 0:
                        eng.wait_ge(bias_ready, 1)
                    elif known is None:
                        eng.wait_ge(s["x2T"], t.index - 3)
                    else:
                        eng.wait_ge(s["k_copied"], known)
                        if known >= 4:
                            eng.wait_ge(s["oT"], known - 3)
                            eng.wait_ge(s["x2T"], known - 3)
                    eng.transpose(act_bank[:, 0:P], xn1[:, t.ring, :], ident[:, :])
                    eng.transpose(act_bank[0:d_ctx, P:2 * P], ctx_sb[:, t.ring, :],
                                  ident[:, :]).then_inc(s["xc_turned"], 1)
                t = stage(at, 4)
                if t:
                    eng.wait_ge(s["x2T"], t.index + 1)
                    eng.wait_ge(s["x1"], t.index + 1)
                    if after_first(t):
                        eng.wait_ge(s["capped"], t.index)
                    if known == 4:
                        eng.wait_ge(small_weights, 16 * 8)
                    eng.matmul(out_bank[:, P:P + experts], x2T[:, t.ring, :], wr_sb[:, :], start=True,
                               stop=True).then_inc(s["logits"], 1)
                t = stage(at, 3)
                if t:
                    eng.wait_ge(s["o_norm"], t.index + 1)
                    if known is None:
                        eng.wait_ge(s["xc_copied"], t.index + 4)
                    else:
                        eng.wait_ge(s["xc_copied"], min(known + 1, tiles))
                        eng.wait_ge(s["k_copied"], min(known, tiles))
                        if known >= 4:
                            eng.wait_ge(s["x2T"], known - 3)
                    eng.sem_inc(pe_waited, 1)
                    for b in range(2):
                        mm = eng.transpose(act_bank[0:PAIRS * d_head, b * P:(b + 1) * P],
                                           o_norm[:, t.ring, b, :, :].rearrange("p h k -> p (h k)"), ident[:, :])
                    mm.then_inc(s["o_turned"], 1)
                t = stage(at, 0)
                if t:
                    eng.wait_ge(s["xc_copied"], t.index + 1)
                    if after_first(t):
                        eng.wait_ge(s["v_copied"], t.index)
                    eng.matmul(qv_bank[:, 0:P], wq_sb[:, :], xT[:, t.ring, :], start=True,
                               stop=True).then_inc(s["q"], 1)
                    if known is None:
                        eng.wait_ge(s["oT"], t.index - 2)
                    elif known >= 3:
                        eng.wait_ge(s["oT"], known - 2)
                    eng.matmul(act_bank[:, 2 * P:3 * P], wk_sb[:, :], cT[:, t.ring, :], start=True,
                               stop=True).then_inc(s["k"], 1)
                t = stage(at, 4)
                if t:
                    eng.wait_ge(s["onehot"], t.index + 1)
                    eng.wait_ge(s["minus_top"], t.index + 1)
                    eng.wait_ge(s["taken"], t.index + 1)
                    eng.matmul(out_bank[:, 144:144 + TOP * experts], tri[:, :],
                               onehot[:, t.ring, :, :].rearrange("p k e -> p (k e)"), start=True, stop=False)
                    eng.matmul(out_bank[:, 144:144 + TOP * experts], ones[:, :],
                               taken[:, t.ring, :, :].rearrange("p k e -> p (k e)"), start=False,
                               stop=True).then_inc(s["ranks"], 1)
                t = stage(at, 3)
                if t:
                    eng.wait_ge(s["oT"], t.index + 1)
                    if known == 3:
                        eng.wait_ge(small_weights, 16 * 8)
                    if after_first(t):
                        eng.wait_ge(s["capped"], t.index)
                        eng.wait_ge(s["x1"], t.index)
                    for j in range(2):
                        mm = eng.matmul(out_bank[:, 0:P], oT[:, t.ring, j, :], wo_sb[:, j, :],
                                        start=(j == 0), stop=(j == 1))
                    mm.then_inc(s["projected"], 1)
                t = stage(at, 2)
                if t:
                    eng.wait_ge(s["v_copied"], t.index + 1)
                    if after_first(t):
                        eng.wait_ge(s["o_norm"], t.index)
                    for p in range(PAIRS):
                        if p % 4 == 0:
                            eng.wait_ge(s["probsT"], t.index * 2 + p // 4 + 1)
                        mm = eng.matmul(o_bank[:, p * 4 * v_cols:(p + 1) * 4 * v_cols], probsT[:, t.ring, p, :],
                                        Vbd[:, t.ring, p].rearrange("p b j k -> p (b j k)"), start=True, stop=True)
                    mm.then_inc(s["pv"], 1)

            run_steps(eng, step)

            def turn_rows(e):
                eng.wait_ge(xg_loaded[e.ring], 16 * (e.half + 1))
                if after_first(e):
                    eng.wait_ge(xgT_ready, e.index)
                for c in range(slot_tiles):
                    mm = eng.transpose(bank[6 + c // 4][:, (c % 4) * P:(c % 4 + 1) * P], xg[:, e.ring, c, 0:d_model],
                                       ident[:, :])
                mm.then_inc(xg_turned, 1)

            def up(e, f):
                if f == 0:
                    eng.wait_ge(xgT_ready, e.index + 1)
                    eng.wait_ge(w1_loaded[e.ring], 16 * (e.half + 1))
                if f >= 2 or after_first(e):
                    eng.wait_ge(gelu_done, e.index * f_tiles + f - 1)
                for h in range(2):
                    mm = eng.matmul(bank[2 * (f % 2) + h][:, 0:capacity], w1_sb[:, e.ring, f * P:(f + 1) * P],
                                    xgT[:, e.ring, h * capacity:(h + 1) * capacity], start=True, stop=True)
                mm.then_inc(up_done, 1)

            def down(e, c):
                if c == 0:
                    eng.wait_ge(gelu_done, (e.index + 1) * f_tiles)
                    eng.wait_ge(w2_loaded[e.ring], 16 * (e.half + 1))
                    if after_first(e):
                        eng.wait_ge(y_biased, e.index)
                for f in range(f_tiles):
                    mm = eng.matmul(bank[4 + c // 4][:, (c % 4) * P:(c % 4 + 1) * P],
                                    hT[:, e.ring, f, c * P:(c + 1) * P], w2_sb[:, e.ring, f, :],
                                    start=(f == 0), stop=(f == f_tiles - 1))
                if c == slot_tiles - 1:
                    mm.then_inc(down_done, 1)

            def expert(e, before, after):
                for f in range(f_tiles):
                    up(e, f)
                    if before:
                        down(before, f)
                if before:
                    for c in range(f_tiles, slot_tiles):
                        down(before, c)
                if after:
                    turn_rows(after)

            turn_rows(Tile(0, 0))
            turn_rows(Tile(0, 1))
            expert(Tile(0, 0), None, None)
            expert(Tile(0, 1), Tile(0, 0), Tile(1, 0))
            with eng.Fori(1, experts // 2 - 1) as half:
                expert(Tile(half, 0), Tile(half - 1, 1), Tile(half, 1))
                expert(Tile(half, 1), Tile(half, 0), Tile(half + 1, 0))
            end = experts // 2 - 1
            expert(Tile(end, 0), Tile(end - 1, 1), Tile(end, 1))
            expert(Tile(end, 1), Tile(end, 0), None)
            for c in range(slot_tiles):
                down(Tile(end, 1), c)


_INS = ["x", "ctx_512", "g_xattn", "g_ffn", "L0_xattn_Wq", "L0_xattn_bq", "L0_xattn_Wk", "L0_xattn_bk",
        "L0_xattn_Wv", "L0_xattn_bv", "L0_xattn_Wo", "L0_xattn_bo", "L0_ffn_Wr", "L0_ffn_W1", "L0_ffn_b1",
        "L0_ffn_W2", "L0_ffn_b2"]


def kernel(**inputs):
    import numpy as _np
    import concourse.bacc as _bacc
    from concourse import mybir as _mybir
    from concourse.bass_utils import run_bass_kernel_spmd as _run

    nc = _bacc.Bacc("TRN2", target_bir_lowering=False, num_devices=1)
    arrays, args = {}, []
    for name in _INS:
        a = _np.ascontiguousarray(inputs[name])
        arrays[f"in_{name}_dram"] = a
        args.append(nc.dram_tensor(f"in_{name}_dram", a.shape, _mybir.dt.from_np(a.dtype), kind="ExternalInput").ap())
    shape = tuple(inputs["x"].shape)
    tokens, width = shape[0] * shape[1], shape[2]
    experts = inputs["L0_ffn_W1"].shape[0]
    capacity = max(1, int(tokens * CAPACITY_FACTOR / experts))
    out = nc.dram_tensor("out_0_dram", shape, F32, kind="ExternalOutput").ap()
    slots = nc.dram_tensor("slots", (experts * TOP * capacity, width + 2 * TOP), F32, kind="Internal").ap()
    picked = nc.dram_tensor("picked", (TOP * tokens, width), F32, kind="Internal").ap()
    flamingo_block(nc, *args, out, slots, picked)
    r = _run(nc, [arrays], core_ids=[0])
    return r.results[0]["out_0_dram"]
```

```python
from contextlib import ExitStack

import concourse.bass as bass
from concourse import mybir

F32 = mybir.dt.float32
BF16 = mybir.dt.bfloat16
I32 = mybir.dt.int32
U32 = mybir.dt.uint32
ACT = mybir.ActivationFunctionType
ALU = mybir.AluOpType
AX = mybir.AxisListType

P = 128
HEADS = 16
PAIRS = HEADS // 2
STRIPS = 4
TOP = 2
CAPACITY_FACTOR = 1.25
LN_EPS = 1e-5
OUT_OF_BOUNDS = 1e6
LAST_PAIRS = 2
LAST_LAG = 6
WARM_STEPS = LAST_LAG + 2


class Tile:

    def __init__(self, half, ring):
        self.half, self.ring = half, ring
        self.index = half * 2 + ring


def tile_at(step_half, step_ring, lag):
    offset = step_ring - lag
    return Tile(step_half + offset // 2, offset % 2)


def flamingo_block(nc, x, ctx_in, g_xattn, g_ffn, wq, bq, wk, bk, wv, bv, wo, bo, wr, w1, b1, w2, b2,
                   out, slots, sums):
    batches, seq, d_model = x.shape
    d_ctx = ctx_in.shape[2]
    tokens = batches * seq
    tiles = tokens // P
    d_head = d_model // HEADS
    experts, _, d_ff = w1.shape
    f_tiles = d_ff // P
    capacity = max(1, int(tokens * CAPACITY_FACTOR / experts))
    per_expert = TOP * capacity
    slot_tiles = per_expert // P
    first_tiles, first_rest = divmod(capacity, P)
    n_slots = experts * per_expert
    row = d_model + 2 * TOP
    dest_at, weight_at = d_model, d_model + TOP
    v_cols = 2 * d_head + 1
    scale = 1.0 / float(d_head) ** 0.5
    assert (d_model, seq, d_head, tiles % 2) == (P, 64, 8, 0) and per_expert % P == 0
    assert slots.shape == (n_slots, row) and sums.shape == (tokens + per_expert, d_model)

    x_tiles = x.rearrange("(t b) s d -> (b s) t d", b=2)
    ctx_tiles = ctx_in.rearrange("(t b) s d -> (b s) t d", b=2)
    out_tiles = out.rearrange("(t b) s d -> (b s) t d", b=2)
    slot_rows = slots.rearrange("(e c p) w -> e p c w", p=P, c=slot_tiles)
    slot_tails = slots.rearrange("(n p) w -> p n w", p=P)
    sum_tiles = sums[0:tokens, :].rearrange("(t p) d -> p t d", p=P)
    spare_rows = sums[tokens:tokens + per_expert, :].rearrange("(c p) d -> p c d", p=P)

    with ExitStack() as stack:
        def sb(name, shape, dtype=F32):
            return stack.enter_context(nc.sbuf_tensor(name, shape, dtype))

        def sem(name):
            return stack.enter_context(nc.semaphore(name))

        x_sb = sb("x_sb", [P, tiles, d_model])
        ctx_sb = sb("ctx_sb", [P, 2, d_ctx])
        wq_sb = sb("wq_sb", [d_model, d_model])
        wk_sb = sb("wk_sb", [d_ctx + 1, d_model])
        wv_sb = sb("wv_sb", [d_ctx + 1, d_model])
        wo_sb = sb("wo_sb", [d_model, d_model])
        wo_own = sb("wo_own", [d_model, 2, d_model])
        wr_sb = sb("wr_sb", [d_model, experts])
        bias_rows = sb("bias_rows", [experts * f_tiles, P])
        bias_cols = sb("bias_cols", [P, experts * f_tiles])
        bq_col = sb("bq_col", [P, 1])
        bq_scaled = sb("bq_scaled", [P, 1])
        bo_all = sb("bo_all", [P, d_model])
        b2_all = sb("b2_all", [P, experts, d_model])
        gates_in = sb("gates_in", [P, 2])
        gates = sb("gates", [P, 2])
        ident = sb("ident", [P, P])
        tri = sb("tri", [P, P], BF16)
        ones = sb("ones", [P, P], BF16)
        band = sb("band", [P, HEADS])
        head_mask = sb("head_mask", [P, STRIPS])
        parity = sb("parity", [P, 2])
        expert_ids = sb("expert_ids", [P, experts])
        slot_base = sb("slot_base", [P, TOP, experts])
        over = sb("over", [P, TOP, experts])
        dest_ids = sb("dest_ids", [P, tiles, TOP])
        minus_half = sb("minus_half", [P, 2])
        eps = sb("eps", [P, 2])
        blank = sb("blank", [P, slot_tiles, row])

        stats1 = sb("stats1", [P, 6])
        stats2 = sb("stats2", [P, 6])
        mv = sb("mv", [P, 2, 2, 2])
        var = sb("var", [P, 2])
        rstd = sb("rstd", [P, 2, 2])
        xn1 = sb("xn1", [P, d_model])
        turned = sb("turned", [P, 2, 4, P])
        X_AT, O_AT, X2_AT = 0, 1, 3
        cT = sb("cT", [d_ctx + 1, 2, P])
        qT = sb("qT", [P, 2, P])
        Qm = sb("Qm", [P, 2, 2, STRIPS, seq])
        Km = sb("Km", [P, 2, 2, STRIPS, seq])
        Vbd = sb("Vbd", [P, 2, PAIRS, 2, v_cols])
        x_res = sb("x_res", [P, tiles, d_model])
        row_max = sb("row_max", [P, 2, 2, STRIPS])
        probs = sb("probs", [P, 2, PAIRS, 2, seq])
        probsT = sb("probsT", [P, 2, PAIRS, P])
        denom = sb("denom", [P, PAIRS, 2])
        o_norm = sb("o_norm", [P, 2, PAIRS, 2 * d_head])
        rows = sb("rows", [P, 2, row])
        top8 = sb("top8", [P, 2, 8])
        top8_at = sb("top8_at", [P, 8], U32)
        minus_top = sb("minus_top", [P, 2])
        onehot = sb("onehot", [P, 2, TOP, experts], BF16)
        taken = sb("taken", [P, 2, TOP, experts], BF16)
        over_cap = sb("over_cap", [P, TOP, experts])
        based = sb("based", [P, TOP, experts])
        at_any = sb("at_any", [P, TOP, experts])
        at_own = sb("at_own", [P, TOP, experts])
        slot_at = sb("slot_at", [P, 2, TOP], I32)
        top_exp = sb("top_exp", [P, 2, TOP])
        top_sum = sb("top_sum", [P, 2])
        top_inv = sb("top_inv", [P, 1])

        w1_sb = sb("w1_sb", [P, 2, d_ff])
        w2_sb = sb("w2_sb", [P, 2, f_tiles, d_model])
        xg = sb("xg", [P, 2, slot_tiles, d_model])
        xgT = sb("xgT", [P, 2, per_expert])
        hT = sb("hT", [P, 2, f_tiles, per_expert])
        tails = sb("tails", [P, experts * slot_tiles, 2 * TOP])
        all_w = sb("all_w", [P, experts, slot_tiles])
        all_dest = sb("all_dest", [P, experts, slot_tiles], I32)
        slot_w = sb("slot_w", [P, 2, slot_tiles])
        slot_dest = sb("slot_dest", [P, 2, slot_tiles], I32)
        y_plus = sb("y_plus", [P, 2, d_model])
        y_sb = sb("y_sb", [P, 2, slot_tiles, d_model])

        bank = [stack.enter_context(nc.psum_tensor(f"bank{i}", [P, 512], F32)) for i in range(8)]
        score_bank = bank[0:2]
        turn_bank = bank[2:4]
        o_bank = bank[4]
        act_bank = bank[5]
        qkv_bank = bank[6]
        out_bank = bank[7]

        x_loaded = [sem(f"x_loaded{i}") for i in range(3)]
        ctx_loaded = [sem(f"ctx_loaded{i}") for i in range(2)]
        attn_weights = sem("attn_weights")
        b1_loaded = sem("b1_loaded")
        gates_loaded = sem("gates_loaded")
        small_weights = sem("small_weights")
        b2_loaded = sem("b2_loaded")
        blank_ready = sem("blank_ready")
        blanked = sem("blanked")
        sums_begun = sem("sums_begun")
        pool_const = sem("pool_const")
        pool_mask = sem("pool_mask")
        dve_const = sem("dve_const")
        bias_turned = sem("bias_turned")
        bias_ready = sem("bias_ready")
        gate_ready = sem("gate_ready")
        gated_bo = sem("gated_bo")
        wo_masked = sem("wo_masked")
        bq_ready = sem("bq_ready")
        names = ["stats1", "mv1", "stats2", "mv2", "var", "rstd", "xn1", "xn2", "turned", "turns_copied", "qkv",
                 "q_copied", "k_copied", "v_copied", "q_masked", "x_bo", "scores", "maxima", "shifted", "probs_turned",
                 "probsT", "pv", "recips", "o_norm", "projected", "x1", "logits", "top8", "top8_at", "minus_top",
                 "onehot", "taken", "ranks", "capped", "at_any", "at_own", "slot_at", "top_exp", "top_inv", "weights",
                 "dests"]
        s = {n: sem("s_" + n) for n in names}
        scattered = [sem(f"scattered{i}") for i in range(2)]
        w1_loaded = [sem(f"w1_loaded{i}") for i in range(2)]
        w2_loaded = [sem(f"w2_loaded{i}") for i in range(2)]
        xg_loaded = [sem(f"xg_loaded{i}") for i in range(2)]
        xg_turned = sem("xg_turned")
        xgT_ready = sem("xgT_ready")
        tails_loaded = sem("tails_loaded")
        tails_picked = sem("tails_picked")
        slot_fields = sem("slot_fields")
        up_done = sem("up_done")
        gelu_done = sem("gelu_done")
        down_done = sem("down_done")
        y_biased = sem("y_biased")
        y_ready = sem("y_ready")
        y_stored = [sem(f"y_stored{i}") for i in range(2)]
        stored = sem("stored")
        dve_waited = sem("dve_waited")
        pe_waited = sem("pe_waited")
        pool_waited = sem("pool_waited")

        block = stack.enter_context(nc.Block())

        def run_steps(eng, step):
            for n in range(WARM_STEPS):
                step(n // 2, n % 2, n)
            with eng.Fori(WARM_STEPS // 2, tiles // 2) as half:
                step(half, 0, None)
                step(half, 1, None)
            for n in range(tiles, tiles + LAST_LAG):
                step(n // 2, n % 2, n)

        def stage(step, lag):
            half, ring, known = step
            if known is not None and not 0 <= known - lag < tiles:
                return None
            return tile_at(half, ring, lag)

        def reused(tile):
            return not isinstance(tile.index, int) or tile.index >= 2

        def after_first(tile):
            return not isinstance(tile.index, int) or tile.index >= 1

        x_pieces = [(0, 2), (2, WARM_STEPS), (WARM_STEPS, tiles)]

        def wait_pieces(eng, tile, pieces, loaded):
            for (a, b), piece_loaded in zip(pieces, loaded):
                if not isinstance(tile.index, int) or a <= tile.index < b:
                    eng.wait_ge(piece_loaded, 16)

        @block.sync
        def _(eng):
            def load_x(i):
                a, b = x_pieces[i]
                eng.dma_start(x_sb[:, a:b, :], x_tiles[:, a:b, :]).then_inc(x_loaded[i], 16)

            def load_ctx(t):
                eng.dma_start(ctx_sb[:, t.ring, :], ctx_tiles[:, t.index, :]).then_inc(ctx_loaded[t.ring], 16)

            def as_row(vector):
                return vector.rearrange("(a n) -> a n", a=1)

            load_x(0)
            load_ctx(Tile(0, 0))
            eng.dma_start(wq_sb[:, :], wq).then_inc(attn_weights, 16)
            eng.dma_start(bq_col[:, :], bq.rearrange("(n a) -> n a", a=1)).then_inc(attn_weights, 16)
            eng.dma_start(wk_sb[0:d_ctx, :], wk).then_inc(attn_weights, 16)
            eng.dma_start(wk_sb[d_ctx:d_ctx + 1, :], as_row(bk)).then_inc(attn_weights, 16)
            eng.dma_start(wv_sb[0:d_ctx, :], wv).then_inc(attn_weights, 16)
            eng.dma_start(wv_sb[d_ctx:d_ctx + 1, :], as_row(bv)).then_inc(attn_weights, 16)
            load_x(1)
            load_ctx(Tile(0, 1))
            eng.dma_start(gates_in[:, 0:1], g_xattn.partition_broadcast(P)).then_inc(gates_loaded, 16)
            eng.dma_start(gates_in[:, 1:2], g_ffn.partition_broadcast(P)).then_inc(gates_loaded, 16)
            load_x(2)
            eng.dma_start(bo_all[:, :], bo.partition_broadcast(P)).then_inc(small_weights, 16)
            eng.dma_start(wo_sb[:, :], wo).then_inc(small_weights, 16)
            eng.dma_start(wr_sb[:, :], wr).then_inc(small_weights, 16)
            eng.dma_start(bias_rows[:, :], b1.rearrange("e (f p) -> (e f) p", p=P)).then_inc(b1_loaded, 16)

            def next_ctx(t):
                eng.wait_ge(s["turned"], t.index - 1)
                load_ctx(t)

            eng.wait_ge(blank_ready, 1)
            early = 4
            for i in range(early):
                next_ctx(Tile(1 + i // 2, i % 2))
                for e in range(i * experts // early, (i + 1) * experts // early):
                    eng.dma_start(slot_rows[e], blank[:, :, :]).then_inc(blanked, 16)
            eng.dma_start(spare_rows, blank[:, :, 0:d_model]).then_inc(sums_begun, 16)
            with eng.Fori(3, tiles // 2) as half:
                for ring in range(2):
                    next_ctx(Tile(half, ring))
            for e in range(2):
                eng.dma_start(w1_sb[:, e, :], w1[e]).then_inc(w1_loaded[e], 16)
                eng.dma_start(w2_sb[:, e, :, :], w2[e].rearrange("(f p) d -> p f d", p=P)).then_inc(w2_loaded[e], 16)
            eng.dma_start(b2_all[:, :, :], b2.rearrange("e d -> (e d)").partition_broadcast(P)).then_inc(b2_loaded, 16)

            for ring in range(2):
                eng.wait_ge(scattered[ring], 16 * TOP * (tiles // 2))
            for e in range(2):
                eng.dma_start(xg[:, e, :, :], slot_rows[e][:, :, 0:d_model]).then_inc(xg_loaded[e], 16)
            eng.dma_start(tails[:, :, :], slot_tails[:, :, d_model:row]).then_inc(tails_loaded, 16)
            def load_slots(e):
                eng.wait_ge(xg_turned, e.index - 1)
                eng.dma_start(xg[:, e.ring, :, :], slot_rows[e.index][:, :, 0:d_model]).then_inc(xg_loaded[e.ring], 16)

            def load_expert(e, after):
                eng.wait_ge(up_done, f_tiles * (e.index - 1))
                eng.dma_start(w1_sb[:, e.ring, :], w1[e.index]).then_inc(w1_loaded[e.ring], 16)
                if after:
                    load_slots(after)
                eng.wait_ge(down_done, slot_tiles * (e.index - 1))
                eng.dma_start(w2_sb[:, e.ring, :, :],
                              w2[e.index].rearrange("(f p) d -> p f d", p=P)).then_inc(w2_loaded[e.ring], 16)

            eng.dma_start(sum_tiles, x_res[:, :, :]).then_inc(sums_begun, 16)
            load_slots(Tile(1, 0))
            with eng.Fori(1, experts // 2 - 1) as half:
                load_expert(Tile(half, 0), Tile(half, 1))
                load_expert(Tile(half, 1), Tile(half + 1, 0))
            load_expert(Tile(experts // 2 - 1, 0), Tile(experts // 2 - 1, 1))
            load_expert(Tile(experts // 2 - 1, 1), None)

            for ring in range(2):
                eng.wait_ge(y_stored[ring], 16 * slot_tiles * (experts // 2))
            eng.dma_start(out.rearrange("b s d -> (b s) d"), sums[0:tokens, :]).then_inc(stored, 16)
            eng.wait_ge(stored, 16)

        @block.gpsimd
        def _(eng):
            eng.memset(ident[:, :], 0.0).then_inc(pool_const, 1)
            eng.memset(ones[:, :], 1.0).then_inc(pool_const, 1)
            eng.memset(minus_half[:, :], -0.5).then_inc(pool_const, 1)
            eng.memset(eps[:, :], LN_EPS)
            eng.memset(band[:, :], 1.0).then_inc(pool_const, 1)
            eng.wait_ge(pool_const, 4)
            eng.affine_select(out=ident[:, :], in_=ident[:, :], compare_op=ALU.not_equal, fill=1.0, base=0,
                              pattern=[[-1, P]], channel_multiplier=1).then_inc(pool_const, 1)
            eng.affine_select(out=band[:, :], in_=band[:, :], compare_op=ALU.is_ge, fill=0.0, base=0,
                              pattern=[[-d_head, HEADS]], channel_multiplier=1).then_inc(pool_const, 1)
            eng.wait_ge(pool_const, 6)
            eng.affine_select(out=band[:, :], in_=band[:, :], compare_op=ALU.is_ge, fill=0.0, base=d_head - 1,
                              pattern=[[d_head, HEADS]], channel_multiplier=-1).then_inc(pool_const, 1)
            eng.affine_select(out=tri[:, :], in_=ones[:, :], compare_op=ALU.is_ge, fill=0.0, base=0,
                              pattern=[[1, P]], channel_multiplier=-1).then_inc(pool_const, 1)
            eng.iota(expert_ids[:, :], pattern=[[1, experts]], base=0, channel_multiplier=0,
                     allow_small_or_imprecise_dtypes=True).then_inc(pool_const, 1)
            eng.iota(slot_base[:, :, :], pattern=[[capacity, TOP], [per_expert, experts]], base=-1,
                     channel_multiplier=0, allow_small_or_imprecise_dtypes=True).then_inc(pool_const, 1)
            eng.iota(dest_ids[:, :, :], pattern=[[P, tiles], [0, TOP]], base=0, channel_multiplier=1,
                     allow_small_or_imprecise_dtypes=True).then_inc(pool_const, 1)
            eng.memset(over[:, :, :], OUT_OF_BOUNDS).then_inc(pool_const, 1)
            eng.memset(taken[:, 0, :, :], 0.0).then_inc(s["taken"], 1)
            eng.memset(blank[:, :, 0:dest_at], 0.0)
            eng.memset(blank[:, :, weight_at:row], 0.0)
            eng.iota(blank[:, :, dest_at:dest_at + TOP], pattern=[[P, slot_tiles], [0, TOP]], base=tokens,
                     channel_multiplier=1, allow_small_or_imprecise_dtypes=True).then_inc(blank_ready, 1)

            x_parts = [slice(tiles * i // 2, tiles * (i + 1) // 2) for i in range(2)]

            def step(half, ring, known):
                at = (half, ring, known)
                t = stage(at, 6)
                if t:
                    if known == 6:
                        eng.wait_ge(blanked, 16 * experts)
                    eng.wait_ge(s["slot_at"], t.index + 1)
                    eng.wait_ge(s["weights"], t.index + 1)
                    eng.wait_ge(s["dests"], t.index + 1)
                    eng.sem_inc(pool_waited, 1)
                    for k in range(TOP):
                        eng.indirect_dma_start(
                            out=slots[:, :], out_offset=bass.IndirectOffsetOnAxis(ap=slot_at[:, t.ring, k:k + 1], axis=0),
                            in_=rows[:, t.ring, :], in_offset=None, bounds_check=n_slots - 1,
                            oob_is_err=False).then_inc(scattered[t.ring], 16)
                t = stage(at, 5)
                if t:
                    if reused(t):
                        eng.wait_ge(scattered[t.ring], 16 * TOP * t.half)
                    eng.tensor_copy(rows[:, t.ring, dest_at:dest_at + TOP],
                                    dest_ids[:, t.index, :]).then_inc(s["dests"], 1)
                t = stage(at, 1)
                if t:
                    eng.wait_ge(s["q_copied"], t.index + 1)
                    if known == 1:
                        eng.wait_ge(pool_mask, 1)
                    if reused(t):
                        eng.wait_ge(s["scores"], t.index * 2 - 2)
                    for b in range(2):
                        last = eng.tensor_tensor(
                            Qm[:, t.ring, b, :, :],
                            qT[:, t.ring, b * seq:(b + 1) * seq].unsqueeze(1).broadcast_to([P, STRIPS, seq]),
                            head_mask[:, :].unsqueeze(2).broadcast_to([P, STRIPS, seq]), ALU.mult)
                    last.then_inc(s["q_masked"], 1)
                t = stage(at, 5)
                if t:
                    eng.wait_ge(s["onehot"], t.index + 1)
                    eng.wait_ge(s["taken"], t.index + 1)
                    if after_first(t):
                        eng.wait_ge(s["ranks"], t.index)
                    eng.tensor_tensor(taken[:, 1 - t.ring, :, :], taken[:, t.ring, :, :], onehot[:, t.ring, :, :],
                                      ALU.add).then_inc(s["taken"], 1)
                first, second = stage(at, 0), stage(at, 4)
                if first or second:
                    t = first or second
                    if first:
                        eng.wait_ge(s["mv1"], first.index + 1)
                    if second:
                        eng.wait_ge(s["mv2"], second.index + 1)
                    now = Tile(half, ring).index
                    if known is None or known >= 1:
                        eng.wait_ge(s["rstd"], now)
                    if known == 0:
                        eng.wait_ge(dve_const, 3)
                    eng.tensor_tensor(var[:, :], mv[:, t.ring, :, 1], eps[:, :], ALU.add).then_inc(s["var"], 1)
                    eng.wait_ge(s["var"], now + 1)
                    if known is None or known >= 2:
                        eng.wait_ge(s["xn1"], now - 1 if known is None else min(now - 1, tiles))
                    if known is None or known >= 6:
                        eng.wait_ge(s["xn2"], now - 5)
                    eng.tensor_tensor(rstd[:, t.ring, :], var[:, :], minus_half[:, :],
                                      ALU.pow).then_inc(s["rstd"], 1)
                if known in (2, 3):
                    if known == 2:
                        eng.wait_ge(gated_bo, 1)
                        for piece in x_loaded:
                            eng.wait_ge(piece, 16)
                    part = x_parts[known - 2]
                    eng.tensor_tensor(x_res[:, part, :], x_sb[:, part, :],
                                      bo_all[:, :].unsqueeze(1).broadcast_to([P, part.stop - part.start, d_model]),
                                      ALU.add).then_inc(s["x_bo"], 1)

            run_steps(eng, step)

            def send_rows(e):
                eng.wait_ge(slot_fields, e.index + 1)
                eng.wait_ge(sums_begun, 32)
                if after_first(e):
                    last = 1 - e.ring
                    eng.wait_ge(y_stored[last], 16 * slot_tiles * (e.half + e.ring))
                for c in range(slot_tiles):
                    eng.wait_ge(y_ready, slot_tiles * e.index + c + 1)
                    eng.sem_inc(pool_waited, 1)
                    eng.indirect_dma_start(
                        out=sums[:, :], out_offset=bass.IndirectOffsetOnAxis(ap=slot_dest[:, e.ring, c:c + 1], axis=0),
                        in_=y_sb[:, e.ring, c, :], in_offset=None, bounds_check=tokens + per_expert - 1,
                        compute_op=ALU.add).then_inc(y_stored[e.ring], 16)

            send_rows(Tile(0, 0))
            send_rows(Tile(0, 1))
            with eng.Fori(1, experts // 2) as half:
                for ring in range(2):
                    send_rows(Tile(half, ring))

        @block.scalar
        def _(eng):
            eng.wait_ge(attn_weights, 16 * 6)
            eng.activation(bq_scaled[:, :], bq_col[:, :], ACT.Copy, scale=scale).then_inc(bq_ready, 1)
            eng.wait_ge(bq_ready, 1)

            def step(half, ring, known):
                at = (half, ring, known)
                x_tile, o_tile, x2_tile = stage(at, 1), stage(at, 4), stage(at, 5)
                if x_tile or o_tile or x2_tile:
                    eng.wait_ge(s["turned"], half * 2 + ring)
                    if known is None or known >= 7:
                        eng.wait_ge(s["logits"], half * 2 + ring - 6)
                    elif known == 6:
                        eng.wait_ge(s["projected"], 1)
                    elif known >= 3:
                        eng.wait_ge(s["qkv"], known - 2)
                    begin = X_AT if x_tile else O_AT if o_tile else X2_AT
                    end = X2_AT + 1 if x2_tile else X2_AT if o_tile else O_AT
                    last = eng.activation(turned[:, ring, begin:end, :], act_bank[:, begin * P:end * P], ACT.Copy)
                    if x_tile:
                        if known == 1:
                            eng.wait_ge(dve_const, 3)
                        last = eng.activation(cT[0:d_ctx, ring, :], o_bank[0:d_ctx, 3 * P:4 * P], ACT.Copy)
                    last.then_inc(s["turns_copied"], 1)
                t = stage(at, 3)
                if t:
                    for h in range(2):
                        eng.wait_ge(s["probs_turned"], t.index * 2 + h + 1)
                        if reused(t):
                            eng.wait_ge(s["pv"], t.index - 1)
                        eng.activation(probsT[:, t.ring, 4 * h:4 * h + 4, :],
                                       turn_bank[h][:, :], ACT.Exp).then_inc(s["probsT"], 1)
                t = stage(at, 1)
                if t:
                    eng.wait_ge(s["qkv"], t.index + 1)
                    if reused(t):
                        eng.wait_ge(s["q_masked"], t.index - 1)
                    eng.activation(qT[:, t.ring, :], qkv_bank[:, 0:P], ACT.Identity, bias=bq_scaled[:, 0:1],
                                   scale=scale).then_inc(s["q_copied"], 1)
                    if reused(t):
                        eng.wait_ge(s["scores"], t.index * 2 - 2)
                    for j in range(STRIPS):
                        r = slice(32 * j, 32 * j + 32)
                        last = eng.activation(Km[r, t.ring, :, j, :],
                                              qkv_bank[r, P:2 * P].rearrange("p (b k) -> p b k", b=2), ACT.Copy)
                    last.then_inc(s["k_copied"], 1)
                t = stage(at, 5)
                if t:
                    eng.wait_ge(s["minus_top"], t.index + 1)
                    if reused(t):
                        eng.wait_ge(s["weights"], t.index - 1)
                    eng.activation(top_exp[:, t.ring, :], top8[:, t.ring, 0:TOP], ACT.Exp,
                                   bias=minus_top[:, t.ring:t.ring + 1],
                                   accum_out=top_sum[:, t.ring:t.ring + 1]).then_inc(s["top_exp"], 1)
                if known == 2:
                    eng.wait_ge(gates_loaded, 32)
                    eng.activation(gates[:, :], gates_in[:, :], ACT.Tanh).then_inc(gate_ready, 1)
                    eng.wait_ge(bias_turned, 1)
                    eng.activation(bias_cols[:, :], out_bank[:, 0:experts * f_tiles], ACT.Copy).then_inc(bias_ready, 1)
                    eng.wait_ge(bias_ready, 1)
                t = stage(at, 1)
                if t:
                    if reused(t):
                        eng.wait_ge(s["pv"], t.index - 1)
                    for b in range(2):
                        own = slice(64 * b, 64 * b + 64)
                        last = eng.activation(Vbd[own, t.ring, :, b, 0:2 * d_head],
                                              qkv_bank[own, 2 * P:3 * P].rearrange("p (h m) -> p h m", m=2 * d_head),
                                              ACT.Copy)
                    last.then_inc(s["v_copied"], 1)

            run_steps(eng, step)

            def gelus(e):
                for f in range(f_tiles):
                    eng.wait_ge(up_done, e.index * f_tiles + f + 1)
                    if reused(e):
                        eng.wait_ge(down_done, slot_tiles * (e.index - 1))
                    for h in range(2):
                        last = eng.activation(
                            hT[:, e.ring, f, h * capacity:(h + 1) * capacity], bank[2 * (f % 2) + h][:, 0:capacity],
                            ACT.Gelu, bias=bias_cols[:, bass.ds(e.index * f_tiles + f, 1)])
                    last.then_inc(gelu_done, 1)

            gelus(Tile(0, 0))
            gelus(Tile(0, 1))
            with eng.Fori(1, experts // 2) as half:
                for ring in range(2):
                    gelus(Tile(half, ring))

        @block.vector
        def _(eng):
            eng.memset(Km[:, :, :, :, :], 0.0)
            eng.memset(Vbd[:, :, :, :, 0:2 * d_head], 0.0).then_inc(dve_const, 1)
            for b in range(2):
                own = slice(64 * b, 64 * b + 64)
                for c in range(2):
                    last = eng.memset(Vbd[own, :, :, c, 2 * d_head:v_cols], 1.0 if b == c else 0.0)
            last.then_inc(dve_const, 1)
            eng.memset(cT[d_ctx:d_ctx + 1, :, :], 1.0)
            eng.memset(mv[:, :, :, :], 1.0).then_inc(dve_const, 1)
            eng.wait_ge(pool_const, 12)
            eng.tensor_reduce(head_mask[:, :], band[:, :].rearrange("p (s h) -> p h s", h=STRIPS), AX.X,
                              ALU.add)
            eng.tensor_reduce(parity[:, :], band[:, :].rearrange("p (h j) -> p j h", j=2), AX.X,
                              ALU.add).then_inc(pool_mask, 1)
            eng.wait_ge(dve_const, 3)

            def take_stats(t, source, stats, name, aggregated):
                if after_first(t):
                    eng.wait_ge(s[aggregated], t.index)
                eng.sem_inc(dve_waited, 1)
                eng.bn_stats(stats[:, :], source).then_inc(s[name], 1)

            def aggregate(t, stats, which, stats_name, done, readers):
                eng.wait_ge(s[stats_name], t.index + 1)
                if reused(t):
                    eng.wait_ge(s[readers], t.index - 1)
                eng.sem_inc(dve_waited, 1)
                eng.bn_aggr(mv[:, t.ring, which, :], stats[:, :]).then_inc(s[done], 1)

            def normalise(t, source, which, to, done):
                eng.tensor_scalar(to, source, mv[:, t.ring, which, 0:1], rstd[:, t.ring, which:which + 1],
                                  ALU.subtract, ALU.mult).then_inc(s[done], 1)

            def find_maxima(t, b):
                n = t.index * 2 + b
                eng.wait_ge(s["scores"], n + 1)
                if not isinstance(t.index, int) or n >= 2:
                    eng.wait_ge(s["shifted"], n - 1)
                scores = score_bank[b][:, :].rearrange("p (g s k) -> p g s k", g=2, k=seq)
                eng.tensor_reduce(row_max[:, b, :, :], scores, AX.X, ALU.max).then_inc(s["maxima"], 1)

            def shift_scores(t, b):
                eng.wait_ge(s["maxima"], t.index * 2 + b + 1)
                if reused(t):
                    eng.wait_ge(s["probs_turned"], t.index * 2 - 2)
                scores = score_bank[b][:, :].rearrange("p (g s k) -> p g s k", g=2, k=seq)
                eng.tensor_tensor(probs[:, t.ring, :, b, :].rearrange("p (s g) k -> p g s k", g=2), scores,
                                  row_max[:, b, :, :].unsqueeze(3).broadcast_to([P, 2, STRIPS, seq]),
                                  ALU.subtract).then_inc(s["shifted"], 1)

            def step(half, ring, known):
                at = (half, ring, known)
                stats_tile, x_tile, score_tile = stage(at, 0), stage(at, 1), stage(at, 2)
                o_tile, route_tile = stage(at, 4), stage(at, 5)
                o = o_bank[:, 0:PAIRS * 2 * v_cols].rearrange("p (h b m) -> p h b m", b=2, m=v_cols)
                if o_tile:
                    t = o_tile
                    eng.wait_ge(s["pv"], t.index + 1)
                    if after_first(t):
                        eng.wait_ge(s["o_norm"], t.index)
                    eng.reciprocal(denom[:, :, :], o[:, :, :, 2 * d_head]).then_inc(s["recips"], 1)
                if route_tile:
                    t = route_tile
                    eng.wait_ge(s["rstd"], t.index + 5)
                    if reused(t):
                        eng.wait_ge(scattered[t.ring], 16 * TOP * t.half)
                    normalise(t, x_res[:, t.index, :], 1, rows[:, t.ring, 0:d_model], "xn2")
                if x_tile:
                    t = x_tile
                    eng.wait_ge(s["rstd"], t.index + 1)
                    if after_first(t):
                        eng.wait_ge(s["turned"], t.index)
                    normalise(t, x_sb[:, t.index, :], 0, xn1[:, :], "xn1")
                if o_tile:
                    t = o_tile
                    eng.wait_ge(s["recips"], t.index + 1)
                    eng.wait_ge(s["turned"], t.index + 3)
                    eng.tensor_tensor(o_norm[:, :, :, :].rearrange("p b h m -> p h b m"), o[:, :, :, 0:2 * d_head],
                                      denom[:, :, :].unsqueeze(3).broadcast_to([P, PAIRS, 2, 2 * d_head]),
                                      ALU.mult).then_inc(s["o_norm"], 1)
                if score_tile:
                    for b in range(2):
                        find_maxima(score_tile, b)
                    for b in range(2):
                        shift_scores(score_tile, b)
                if stats_tile:
                    t = stats_tile
                    wait_pieces(eng, t, x_pieces, x_loaded)
                    take_stats(t, x_sb[:, t.index, :], stats1, "stats1", "mv1")
                if known == 2:
                    eng.wait_ge(gate_ready, 1)
                    eng.wait_ge(small_weights, 16 * 3)
                    eng.tensor_scalar(bo_all[:, :], bo_all[:, :], gates[:, 0:1], None, ALU.mult).then_inc(gated_bo, 1)
                    eng.wait_ge(pool_mask, 1)
                    for j in range(2):
                        last = eng.tensor_scalar(wo_own[:, j, :], wo_sb[:, :], parity[:, j:j + 1], None, ALU.mult)
                    last.then_inc(wo_masked, 1)
                if stats_tile:
                    aggregate(stats_tile, stats1, 0, "stats1", "mv1", "xn1")
                logits = out_bank[:, P:P + experts]
                if route_tile:
                    t = route_tile
                    eng.wait_ge(s["logits"], t.index + 1)
                    if reused(t):
                        eng.wait_ge(s["top_exp"], t.index - 1)
                    eng.sem_inc(dve_waited, 1)
                    eng.max(top8[:, t.ring, :], logits).then_inc(s["top8"], 1)
                if o_tile:
                    t = o_tile
                    eng.wait_ge(s["projected"], t.index + 1)
                    if known == 4:
                        eng.wait_ge(s["x_bo"], 2)
                    eng.scalar_tensor_tensor(out=x_res[:, t.index, :], in0=out_bank[:, 0:P], scalar=gates[:, 0:1],
                                             in1=x_res[:, t.index, :], op0=ALU.mult, op1=ALU.add).then_inc(s["x1"], 1)
                if route_tile:
                    t = route_tile
                    eng.wait_ge(s["top8"], t.index + 1)
                    if after_first(t):
                        eng.wait_ge(s["onehot"], t.index)
                    eng.sem_inc(dve_waited, 1)
                    eng.max_index(top8_at[:, :], top8[:, t.ring, :], logits).then_inc(s["top8_at"], 1)
                    eng.tensor_scalar(minus_top[:, t.ring:t.ring + 1], top8[:, t.ring, 0:1], -1.0, None,
                                      ALU.mult).then_inc(s["minus_top"], 1)
                if o_tile:
                    t = o_tile
                    eng.wait_ge(s["x1"], t.index + 1)
                    take_stats(t, x_res[:, t.index, :], stats2, "stats2", "mv2")
                if route_tile:
                    t = route_tile
                    eng.wait_ge(s["top8_at"], t.index + 1)
                    if reused(t):
                        eng.wait_ge(s["taken"], t.index)
                        eng.wait_ge(s["ranks"], t.index - 1)
                    eng.tensor_tensor(onehot[:, t.ring, :, :],
                                      expert_ids[:, :].unsqueeze(1).broadcast_to([P, TOP, experts]),
                                      top8_at[:, 0:TOP].unsqueeze(2).broadcast_to([P, TOP, experts]),
                                      ALU.is_equal).then_inc(s["onehot"], 1)
                if o_tile:
                    aggregate(o_tile, stats2, 1, "stats2", "mv2", "xn2")
                if route_tile:
                    t = route_tile
                    rank = out_bank[:, 144:144 + TOP * experts].rearrange("p (k e) -> p k e", k=TOP)
                    eng.wait_ge(s["ranks"], t.index + 1)
                    if after_first(t):
                        eng.wait_ge(s["at_any"], t.index)
                    eng.scalar_tensor_tensor(out=over_cap[:, :, :], in0=rank, scalar=float(capacity),
                                             in1=over[:, :, :], op0=ALU.is_gt, op1=ALU.mult)
                    eng.tensor_tensor(based[:, :, :], rank, slot_base[:, :, :], ALU.add).then_inc(s["capped"], 1)
                    eng.wait_ge(s["top_exp"], t.index + 1)
                    if after_first(t):
                        eng.wait_ge(s["weights"], t.index)
                    eng.reciprocal(top_inv[:, :], top_sum[:, t.ring:t.ring + 1]).then_inc(s["top_inv"], 1)
                    eng.wait_ge(s["capped"], t.index + 1)
                    if after_first(t):
                        eng.wait_ge(s["at_own"], t.index)
                    eng.tensor_tensor(at_any[:, :, :], over_cap[:, :, :], based[:, :, :],
                                      ALU.add).then_inc(s["at_any"], 1)
                    eng.wait_ge(s["top_inv"], t.index + 1)
                    eng.tensor_scalar(rows[:, t.ring, weight_at:weight_at + TOP], top_exp[:, t.ring, :],
                                      top_inv[:, 0:1], gates[:, 1:2], ALU.mult, ALU.mult).then_inc(s["weights"], 1)
                    eng.wait_ge(s["at_any"], t.index + 1)
                    if after_first(t):
                        eng.wait_ge(s["slot_at"], t.index)
                    eng.tensor_tensor(at_own[:, :, :], at_any[:, :, :], onehot[:, t.ring, :, :],
                                      ALU.mult).then_inc(s["at_own"], 1)
                    eng.wait_ge(s["at_own"], t.index + 1)
                    with nc.allow_low_precision(reason="the sum of one whole number and zeros, exact in int32"):
                        eng.tensor_reduce(slot_at[:, t.ring, :], at_own[:, :, :], AX.X,
                                          ALU.add).then_inc(s["slot_at"], 1)

            run_steps(eng, step)

            split = min(512, per_expert)

            def turn_in(e):
                eng.wait_ge(xg_turned, e.index + 1)
                if reused(e):
                    eng.wait_ge(up_done, f_tiles * (e.index - 1))
                eng.tensor_copy(xgT[:, e.ring, 0:split], bank[6][:, 0:split])
                eng.tensor_copy(xgT[:, e.ring, split:per_expert], bank[7][:, 0:per_expert - split]).then_inc(xgT_ready, 1)

            def pick_tails():
                eng.wait_ge(tails_loaded, 16)
                fields = tails[:, :, :].rearrange("p (e c) w -> p e c w", e=experts)
                for to, at in ((all_w, TOP), (all_dest, 0)):
                    eng.tensor_copy(to[:, :, 0:first_tiles], fields[:, :, 0:first_tiles, at])
                    for part, k in ((slice(0, first_rest), 0), (slice(first_rest, P), 1)):
                        eng.tensor_copy(to[part, :, first_tiles], fields[part, :, first_tiles, at + k])
                    last = eng.tensor_copy(to[:, :, first_tiles + 1:slot_tiles],
                                           fields[:, :, first_tiles + 1:slot_tiles, at + 1])
                last.then_inc(tails_picked, 1)
                eng.wait_ge(tails_picked, 1)

            def take_fields(e):
                if reused(e):
                    eng.wait_ge(y_stored[e.ring], 16 * slot_tiles * e.half)
                    eng.wait_ge(y_ready, slot_tiles * (e.index - 1))
                eng.tensor_copy(slot_w[:, e.ring, :].unsqueeze(1), all_w[:, bass.ds(e.index, 1), :])
                eng.tensor_copy(slot_dest[:, e.ring, :].unsqueeze(1),
                                all_dest[:, bass.ds(e.index, 1), :]).then_inc(slot_fields, 1)

            def turn_out(e):
                eng.wait_ge(slot_fields, e.index + 1)
                if reused(e):
                    eng.wait_ge(y_stored[e.ring], 16 * slot_tiles * e.half)
                for c in range(slot_tiles):
                    n = slot_tiles * e.index + c
                    part = (e.ring + c) % 2
                    eng.wait_ge(down_done, n + 1)
                    if not isinstance(n, int) or n >= 2:
                        eng.wait_ge(y_ready, n - 1)
                    eng.tensor_tensor(y_plus[:, part, :].unsqueeze(1), bank[4 + part][:, 0:d_model].unsqueeze(1),
                                      b2_all[:, bass.ds(e.index, 1), :], ALU.add).then_inc(y_biased, 1)
                    eng.wait_ge(y_biased, n + 1)
                    eng.tensor_scalar(y_sb[:, e.ring, c, :], y_plus[:, part, :], slot_w[:, e.ring, c:c + 1], None,
                                      ALU.mult).then_inc(y_ready, 1)

            turn_in(Tile(0, 0))
            turn_in(Tile(0, 1))
            pick_tails()
            take_fields(Tile(0, 0))
            turn_in(Tile(1, 0))
            eng.wait_ge(b2_loaded, 16)
            turn_out(Tile(0, 0))
            take_fields(Tile(0, 1))
            with eng.Fori(1, experts // 2 - 1) as half:
                turn_in(Tile(half, 1))
                turn_out(Tile(half - 1, 1))
                take_fields(Tile(half, 0))
                turn_in(Tile(half + 1, 0))
                turn_out(Tile(half, 0))
                take_fields(Tile(half, 1))
            end = experts // 2 - 1
            turn_in(Tile(end, 1))
            turn_out(Tile(end - 1, 1))
            take_fields(Tile(end, 0))
            turn_out(Tile(end, 0))
            take_fields(Tile(end, 1))
            turn_out(Tile(end, 1))

        @block.tensor
        def _(eng):
            eng.wait_ge(pool_const, 12)
            def step(half, ring, known):
                at = (half, ring, known)
                x_tile, o_tile, route_tile = stage(at, 1), stage(at, 4), stage(at, 5)
                t = stage(at, 2)
                if t:
                    eng.wait_ge(s["q_masked"], t.index + 1)
                    eng.wait_ge(s["k_copied"], t.index + 1)
                    for b in range(2):
                        if after_first(t):
                            eng.wait_ge(s["shifted"], t.index * 2 - 1 + b)
                        for g in range(2):
                            mm = eng.matmul(score_bank[b][:, 256 * g:256 * g + 256],
                                            Qm[:, t.ring, b, 2 * g:2 * g + 2, :].rearrange("p j q -> p (j q)"),
                                            Km[:, t.ring, b, :, :].rearrange("p s k -> p (s k)"),
                                            start=True, stop=True)
                        mm.then_inc(s["scores"], 1)
                if x_tile or o_tile or route_tile:
                    if known is None or known >= 2:
                        eng.wait_ge(s["turns_copied"], half * 2 + ring - 1)
                if route_tile:
                    t = route_tile
                    eng.wait_ge(s["xn2"], t.index + 1)
                    mm = eng.transpose(act_bank[:, X2_AT * P:(X2_AT + 1) * P], rows[:, t.ring, 0:d_model], ident[:, :])
                if o_tile:
                    t = o_tile
                    eng.wait_ge(s["o_norm"], t.index + 1)
                    for b in range(2):
                        mm = eng.transpose(
                            act_bank[:, O_AT * P:(O_AT + 2) * P].rearrange("p (j b q) -> p j b q", j=2, b=2)[:, :, b, :],
                            o_norm[:, b, :, :].rearrange("p h m -> p (h m)"), ident[:, :])
                if x_tile:
                    t = x_tile
                    eng.wait_ge(s["xn1"], t.index + 1)
                    eng.wait_ge(ctx_loaded[t.ring], 16 * (t.half + 1))
                    eng.transpose(act_bank[:, X_AT * P:(X_AT + 1) * P], xn1[:, :], ident[:, :])
                    mm = eng.transpose(o_bank[0:d_ctx, 3 * P:4 * P], ctx_sb[:, t.ring, :], ident[:, :])
                if x_tile or o_tile or route_tile:
                    mm.then_inc(s["turned"], 1)
                t = stage(at, 3)
                if t:
                    eng.wait_ge(s["shifted"], t.index * 2 + 2)
                    for h in range(2):
                        if after_first(t):
                            eng.wait_ge(s["probsT"], t.index * 2 - 1 + h)
                        for i in range(4):
                            p = 4 * h + i
                            mm = eng.transpose(turn_bank[h][:, i * P:(i + 1) * P],
                                               probs[:, t.ring, p, :, :].rearrange("p b k -> p (b k)"), ident[:, :])
                        mm.then_inc(s["probs_turned"], 1)
                if x_tile or o_tile or route_tile:
                    eng.wait_ge(s["turns_copied"], half * 2 + ring)
                if x_tile:
                    t = x_tile
                    if known == 1:
                        eng.wait_ge(attn_weights, 16 * 6)
                    if after_first(t):
                        eng.wait_ge(s["v_copied"], t.index)
                    eng.matmul(qkv_bank[:, 0:P], wq_sb[:, :], turned[:, ring, X_AT, :], start=True, stop=True)
                    eng.matmul(qkv_bank[:, P:2 * P], wk_sb[:, :], cT[:, ring, :], start=True, stop=True)
                    eng.matmul(qkv_bank[:, 2 * P:3 * P], cT[:, ring, :], wv_sb[:, :], start=True,
                               stop=True).then_inc(s["qkv"], 1)
                if known == 2:
                    eng.wait_ge(b1_loaded, 16)
                    n_b1 = experts * f_tiles
                    eng.transpose(out_bank[:, 0:n_b1], bias_rows[:, :], ident[0:n_b1, 0:n_b1]).then_inc(bias_turned, 1)
                if o_tile or route_tile:
                    if known is None or known >= 5:
                        eng.wait_ge(s["x1"], half * 2 + ring - 4 if known is None else min(known - 4, tiles))
                    if known is None or known >= 6:
                        eng.wait_ge(s["capped"], half * 2 + ring - 5)
                if o_tile:
                    if known == 4:
                        eng.wait_ge(wo_masked, 1)
                        eng.wait_ge(bias_ready, 1)
                    for j in range(2):
                        mm = eng.matmul(out_bank[:, 0:P], turned[:, ring, O_AT + j, :], wo_own[:, j, :],
                                        start=(j == 0), stop=(j == 1))
                    mm.then_inc(s["projected"], 1)
                if route_tile:
                    if known == 5:
                        eng.wait_ge(small_weights, 16 * 3)
                    eng.matmul(out_bank[:, P:P + experts], turned[:, ring, X2_AT, :], wr_sb[:, :], start=True,
                               stop=True).then_inc(s["logits"], 1)
                pv_tile = stage(at, 3)

                def weigh_values(pairs):
                    t = pv_tile
                    for p in pairs:
                        if p % 4 == 0:
                            eng.wait_ge(s["probsT"], t.index * 2 + p // 4 + 1)
                        mm = eng.matmul(o_bank[:, p * 2 * v_cols:(p + 1) * 2 * v_cols], probsT[:, t.ring, p, :],
                                        Vbd[:, t.ring, p].rearrange("p b m -> p (b m)"), start=True, stop=True)
                    return mm

                if pv_tile:
                    eng.wait_ge(s["v_copied"], pv_tile.index + 1)
                    eng.wait_ge(s["turns_copied"], pv_tile.index + 3)
                    if after_first(pv_tile):
                        eng.wait_ge(s["o_norm"], pv_tile.index)
                    weigh_values(range(PAIRS - LAST_PAIRS))
                if route_tile:
                    t = route_tile
                    eng.wait_ge(s["onehot"], t.index + 1)
                    eng.wait_ge(s["taken"], t.index + 1)
                    if o_tile:
                        eng.wait_ge(s["x1"], o_tile.index + 1)
                    eng.matmul(out_bank[:, 144:144 + TOP * experts], tri[:, :],
                               onehot[:, t.ring, :, :].rearrange("p k e -> p (k e)"), start=True, stop=False)
                    eng.matmul(out_bank[:, 144:144 + TOP * experts], ones[:, :],
                               taken[:, t.ring, :, :].rearrange("p k e -> p (k e)"), start=False,
                               stop=True).then_inc(s["ranks"], 1)
                if pv_tile:
                    weigh_values(range(PAIRS - LAST_PAIRS, PAIRS)).then_inc(s["pv"], 1)

            run_steps(eng, step)

            def turn_rows(e):
                eng.wait_ge(xg_loaded[e.ring], 16 * (e.half + 1))
                if after_first(e):
                    eng.wait_ge(xgT_ready, e.index)
                for c in range(slot_tiles):
                    mm = eng.transpose(bank[6 + c // 4][:, (c % 4) * P:(c % 4 + 1) * P], xg[:, e.ring, c, 0:d_model],
                                       ident[:, :])
                mm.then_inc(xg_turned, 1)

            def up(e, f):
                if f == 0:
                    eng.wait_ge(xgT_ready, e.index + 1)
                    eng.wait_ge(w1_loaded[e.ring], 16 * (e.half + 1))
                if f >= 2 or after_first(e):
                    eng.wait_ge(gelu_done, e.index * f_tiles + f - 1)
                for h in range(2):
                    mm = eng.matmul(bank[2 * (f % 2) + h][:, 0:capacity], w1_sb[:, e.ring, f * P:(f + 1) * P],
                                    xgT[:, e.ring, h * capacity:(h + 1) * capacity], start=True, stop=True)
                mm.then_inc(up_done, 1)

            def down(e, c):
                if c == 0:
                    eng.wait_ge(gelu_done, (e.index + 1) * f_tiles)
                    eng.wait_ge(w2_loaded[e.ring], 16 * (e.half + 1))
                n = slot_tiles * e.index + c
                if not isinstance(n, int) or n >= 2:
                    eng.wait_ge(y_biased, n - 1)
                for f in range(f_tiles):
                    mm = eng.matmul(bank[4 + (e.ring + c) % 2][:, 0:d_model],
                                    hT[:, e.ring, f, c * P:(c + 1) * P], w2_sb[:, e.ring, f, :],
                                    start=(f == 0), stop=(f == f_tiles - 1))
                mm.then_inc(down_done, 1)

            def expert(e, before, after):
                for f in range(f_tiles):
                    up(e, f)
                    if f == 0 and after:
                        turn_rows(after)
                    if before:
                        down(before, f)
                if before:
                    for c in range(f_tiles, slot_tiles):
                        down(before, c)

            turn_rows(Tile(0, 0))
            expert(Tile(0, 0), None, Tile(0, 1))
            expert(Tile(0, 1), Tile(0, 0), Tile(1, 0))
            with eng.Fori(1, experts // 2 - 1) as half:
                expert(Tile(half, 0), Tile(half - 1, 1), Tile(half, 1))
                expert(Tile(half, 1), Tile(half, 0), Tile(half + 1, 0))
            end = experts // 2 - 1
            expert(Tile(end, 0), Tile(end - 1, 1), Tile(end, 1))
            expert(Tile(end, 1), Tile(end, 0), None)
            for c in range(slot_tiles):
                down(Tile(end, 1), c)


_INS = ["x", "ctx_512", "g_xattn", "g_ffn", "L0_xattn_Wq", "L0_xattn_bq", "L0_xattn_Wk", "L0_xattn_bk",
        "L0_xattn_Wv", "L0_xattn_bv", "L0_xattn_Wo", "L0_xattn_bo", "L0_ffn_Wr", "L0_ffn_W1", "L0_ffn_b1",
        "L0_ffn_W2", "L0_ffn_b2"]


def kernel(**inputs):
    import numpy as _np
    import concourse.bacc as _bacc
    from concourse import mybir as _mybir
    from concourse.bass_utils import run_bass_kernel_spmd as _run

    nc = _bacc.Bacc("TRN2", target_bir_lowering=False, num_devices=1)
    arrays, args = {}, []
    for name in _INS:
        a = _np.ascontiguousarray(inputs[name])
        arrays[f"in_{name}_dram"] = a
        args.append(nc.dram_tensor(f"in_{name}_dram", a.shape, _mybir.dt.from_np(a.dtype), kind="ExternalInput").ap())
    shape = tuple(inputs["x"].shape)
    tokens, width = shape[0] * shape[1], shape[2]
    experts = inputs["L0_ffn_W1"].shape[0]
    capacity = max(1, int(tokens * CAPACITY_FACTOR / experts))
    out = nc.dram_tensor("out_0_dram", shape, F32, kind="ExternalOutput").ap()
    slots = nc.dram_tensor("slots", (experts * TOP * capacity, width + 2 * TOP), F32, kind="Internal").ap()
    sums = nc.dram_tensor("sums", (tokens + TOP * capacity, width), F32, kind="Internal").ap()
    flamingo_block(nc, *args, out, slots, sums)
    r = _run(nc, [arrays], core_ids=[0])
    return r.results[0]["out_0_dram"]
```

```python
from contextlib import ExitStack

import concourse.bass as bass
from concourse import mybir

F32 = mybir.dt.float32
BF16 = mybir.dt.bfloat16
I32 = mybir.dt.int32
U32 = mybir.dt.uint32
ACT = mybir.ActivationFunctionType
ALU = mybir.AluOpType
AX = mybir.AxisListType

P = 128
HEADS = 16
PAIRS = HEADS // 2
STRIPS = 4
TOP = 2
CAPACITY_FACTOR = 1.25
LN_EPS = 1e-5
OUT_OF_BOUNDS = 1e6
LAST_PAIRS = 2
LAST_FILLING = 2
WARM_START, WARM_COPY, WARM_CHOICE, WARM_STEP, WARM_EXPERTS = 9, 2, 2, 4, 20
LAST_LAG = 6
PEELED_STEPS = LAST_LAG + 2


def plus(value, constant):
    return value + constant if constant else value


class Tile:

    def __init__(self, half, offset):
        self.loop_half, self.offset = half, offset
        self.ring = offset % 2

    @property
    def half(self):
        return plus(self.loop_half, self.offset // 2)

    @property
    def index(self):
        return self.plus(0)

    def plus(self, constant):
        return plus(self.loop_half * 2, self.offset + constant)

    def twice(self, constant):
        return plus(self.loop_half * 4, 2 * self.offset + constant)

    def earlier(self, amount):
        return plus(self.loop_half * amount, self.offset // 2 * amount)


def flamingo_block(nc, x, ctx_in, gates_ab, wq_bq, wkv_bkv, wo, bo, wr, w1, b1, w2, b2,
                   out, slots):
    batches, seq, d_model = x.shape
    d_ctx = ctx_in.shape[2]
    tokens = batches * seq
    tiles = tokens // P
    d_head = d_model // HEADS
    experts, _, d_ff = w1.shape
    f_tiles = d_ff // P
    capacity = max(1, int(tokens * CAPACITY_FACTOR / experts))
    per_expert = TOP * capacity
    slot_tiles = per_expert // P
    first_tiles, first_rest = divmod(capacity, P)
    turned_first = -(-capacity // P)
    n_slots = experts * per_expert
    row = d_model + 2 * TOP
    dest_at, weight_at = d_model, d_model + TOP
    v_cols = 2 * d_head + 1
    scale = 1.0 / float(d_head) ** 0.5
    assert (d_model, seq, d_head, tiles % 2) == (P, 64, 8, 0) and per_expert % P == 0
    assert slots.shape == (n_slots, row)

    x_tiles = x.rearrange("(t b) s d -> (b s) t d", b=2)
    ctx_tiles = ctx_in.rearrange("(t b) s d -> (b s) t d", b=2)
    out_tiles = out.rearrange("(t b) s d -> (b s) t d", b=2)
    slot_rows = slots.rearrange("(e c p) w -> e p c w", p=P, c=slot_tiles)
    slot_tails = slots.rearrange("(n p) w -> p n w", p=P)
    out_rows = out.rearrange("b s d -> (b s) d")

    with ExitStack() as stack:
        def sb(name, shape, dtype=F32):
            return stack.enter_context(nc.sbuf_tensor(name, shape, dtype))

        def sem(name):
            return stack.enter_context(nc.semaphore(name))

        x_sb = sb("x_sb", [P, tiles, d_model])
        ctx_sb = sb("ctx_sb", [P, 2, d_ctx])
        wq_sb = sb("wq_sb", [d_model, d_model + 1])
        wkv_sb = sb("wkv_sb", [d_ctx + 1, 2 * d_model])
        wo_sb = sb("wo_sb", [d_model, d_model])
        wo_own = sb("wo_own", [d_model, 2, d_model])
        wr_sb = sb("wr_sb", [d_model, experts])
        bias_rows = sb("bias_rows", [experts * f_tiles, P])
        bias_cols = sb("bias_cols", [P, experts * f_tiles])
        bq_scaled = sb("bq_scaled", [P, 1])
        bo_all = sb("bo_all", [P, d_model])
        b2_all = sb("b2_all", [P, experts, d_model])
        gates_in = sb("gates_in", [P, 2])
        gates = sb("gates", [P, 2])
        ident = sb("ident", [P, P])
        tri = sb("tri", [P, P], BF16)
        ones = sb("ones", [P, P], BF16)
        warm = sb("warm", [P, 4 * P], BF16)
        band = sb("band", [P, HEADS])
        head_mask = sb("head_mask", [P, STRIPS])
        parity = sb("parity", [P, 2])
        expert_ids = sb("expert_ids", [P, experts])
        slot_base = sb("slot_base", [P, TOP, experts])
        over = sb("over", [P, TOP, experts])
        dest_ids = sb("dest_ids", [P, tiles, TOP])
        minus_half = sb("minus_half", [P, 2])
        eps = sb("eps", [P, 2])
        blank = sb("blank", [P, slot_tiles, row])

        stats1 = sb("stats1", [P, 6])
        stats2 = sb("stats2", [P, 6])
        mv = sb("mv", [P, 2, 2, 2])
        var = sb("var", [P, 2])
        rstd = sb("rstd", [P, 2, 2])
        xn1 = sb("xn1", [P, d_model])
        turned = sb("turned", [P, 2, 4, P])
        X_AT, O_AT, X2_AT = 0, 1, 3
        cT = sb("cT", [d_ctx + 1, 2, P])
        qT = sb("qT", [P, 2, P])
        Qm = sb("Qm", [P, 2, 2, STRIPS, seq])
        Km = sb("Km", [P, 2, 2, STRIPS, seq])
        Vbd = sb("Vbd", [P, 2, PAIRS, 2, v_cols])
        x_res = sb("x_res", [P, tiles, d_model])
        row_max = sb("row_max", [P, 2, 2, STRIPS])
        probs = sb("probs", [P, 2, PAIRS, 2, seq])
        probsT = sb("probsT", [P, 2, PAIRS, P])
        denom = sb("denom", [P, PAIRS, 2])
        o_norm = sb("o_norm", [P, 2, PAIRS, 2 * d_head])
        rows = sb("rows", [P, 2, row])
        top8 = sb("top8", [P, 2, 8])
        top8_at = sb("top8_at", [P, 8], U32)
        minus_top = sb("minus_top", [P, 2])
        onehot = sb("onehot", [P, 2, TOP, experts], BF16)
        taken = sb("taken", [P, 2, TOP, experts], BF16)
        over_cap = sb("over_cap", [P, TOP, experts])
        based = sb("based", [P, TOP, experts])
        at_any = sb("at_any", [P, TOP, experts])
        at_own = sb("at_own", [P, TOP, experts])
        slot_at = sb("slot_at", [P, 2, TOP], I32)
        top_exp = sb("top_exp", [P, 2, TOP])
        top_sum = sb("top_sum", [P, 2])
        top_inv = sb("top_inv", [P, 1])

        w1_sb = sb("w1_sb", [P, 2, d_ff])
        w2_sb = sb("w2_sb", [P, 2, f_tiles, d_model])
        xg = sb("xg", [P, 2, slot_tiles, d_model])
        xgT = sb("xgT", [P, 2, per_expert])
        hT = sb("hT", [P, 2, f_tiles, per_expert])
        tails = sb("tails", [P, experts * slot_tiles, 2 * TOP])
        all_w = sb("all_w", [P, experts, slot_tiles])
        all_dest = sb("all_dest", [P, experts, slot_tiles], I32)
        slot_w = sb("slot_w", [P, 2, slot_tiles])
        slot_dest = sb("slot_dest", [P, 2, slot_tiles], I32)
        y_plus = sb("y_plus", [P, 2, d_model])
        y_sb = sb("y_sb", [P, 2, slot_tiles, d_model])

        bank = [stack.enter_context(nc.psum_tensor(f"bank{i}", [P, 512], F32)) for i in range(8)]
        score_bank = bank[0:2]
        turn_bank = bank[2:4]
        o_bank = bank[4]
        act_bank = bank[5]
        qkv_bank = bank[6]
        out_bank = bank[7]

        x_loaded = [sem(f"x_loaded{i}") for i in range(3)]
        ctx_loaded = [sem(f"ctx_loaded{i}") for i in range(2)]
        attn_weights = sem("attn_weights")
        b1_loaded = sem("b1_loaded")
        gates_loaded = sem("gates_loaded")
        small_weights = sem("small_weights")
        b2_loaded = sem("b2_loaded")
        blank_ready = sem("blank_ready")
        blanked = sem("blanked")
        residual_stored = sem("residual_stored")
        pool_const = sem("pool_const")
        warm_ready = sem("warm_ready")
        pool_mask = sem("pool_mask")
        dve_const = sem("dve_const")
        bias_turned = sem("bias_turned")
        bias_ready = sem("bias_ready")
        gate_ready = sem("gate_ready")
        gated_bo = sem("gated_bo")
        wo_masked = sem("wo_masked")
        bq_ready = sem("bq_ready")
        names = ["stats1", "mv1", "stats2", "mv2", "var", "rstd", "xn1", "xn2", "turned", "turns_copied", "qkv",
                 "q_copied", "k_copied", "v_copied", "q_masked", "x_bo", "scores", "maxima", "shifted", "probs_turned",
                 "probsT", "pv", "recips", "o_norm", "projected", "x1", "logits", "top8", "top8_at", "minus_top",
                 "onehot", "taken", "ranks", "capped", "at_any", "at_own", "slot_at", "top_exp", "top_inv", "weights",
                 "dests"]
        s = {n: sem("s_" + n) for n in names}
        scattered = [sem(f"scattered{i}") for i in range(2)]
        w1_loaded = [sem(f"w1_loaded{i}") for i in range(2)]
        w2_loaded = [sem(f"w2_loaded{i}") for i in range(2)]
        xg_loaded = [sem(f"xg_loaded{i}") for i in range(2)]
        first_slots = sem("first_slots")
        xg_turned = sem("xg_turned")
        xgT_ready = sem("xgT_ready")
        tails_loaded = sem("tails_loaded")
        tails_picked = sem("tails_picked")
        slot_fields = sem("slot_fields")
        up_done = sem("up_done")
        gelu_done = sem("gelu_done")
        down_done = sem("down_done")
        y_biased = sem("y_biased")
        y_ready = sem("y_ready")
        y_stored = [sem(f"y_stored{i}") for i in range(2)]
        dve_waited = sem("dve_waited")
        pool_waited = sem("pool_waited")

        block = stack.enter_context(nc.Block())

        def run_steps(eng, step):
            for n in range(PEELED_STEPS):
                step(n // 2, n % 2, n)
            with eng.Fori(PEELED_STEPS // 2, tiles // 2) as half:
                step(half, 0, None)
                step(half, 1, None)
            for n in range(tiles, tiles + LAST_LAG):
                step(n // 2, n % 2, n)

        def stage(step, lag):
            half, ring, known = step
            if known is not None and not 0 <= known - lag < tiles:
                return None
            return Tile(half, ring - lag)

        def reused(tile):
            return not isinstance(tile.index, int) or tile.index >= 2

        def filling(known):
            return known is not None and known <= LAST_FILLING

        def draining(known):
            return known is not None and known > tiles + 1

        def after_first(tile):
            return not isinstance(tile.index, int) or tile.index >= 1

        x_pieces = [(0, 2), (2, PEELED_STEPS), (PEELED_STEPS, tiles)]

        @block.sync
        def _(eng):
            def load_x(i):
                a, b = x_pieces[i]
                eng.dma_start(x_sb[:, a:b, :], x_tiles[:, a:b, :]).then_inc(x_loaded[i], 16)

            def load_ctx(t):
                eng.dma_start(ctx_sb[:, t.ring, :], ctx_tiles[:, t.index, :]).then_inc(ctx_loaded[t.ring], 16)

            load_x(0)
            load_ctx(Tile(0, 0))
            eng.dma_start(wq_sb[:, :], wq_bq).then_inc(attn_weights, 16)
            eng.dma_start(wkv_sb[:, :], wkv_bkv).then_inc(attn_weights, 16)
            load_x(1)
            load_ctx(Tile(0, 1))
            eng.dma_start(gates_in[:, :], gates_ab.partition_broadcast(P)).then_inc(gates_loaded, 16)
            load_x(2)
            eng.dma_start(bo_all[:, :], bo.partition_broadcast(P)).then_inc(small_weights, 16)
            eng.dma_start(wo_sb[:, :], wo).then_inc(small_weights, 16)
            eng.dma_start(wr_sb[:, :], wr).then_inc(small_weights, 16)
            eng.dma_start(bias_rows[:, :], b1.rearrange("e (f p) -> (e f) p", p=P)).then_inc(b1_loaded, 16)

            def next_ctx(t):
                eng.wait_ge(s["turned"], t.plus(-1))
                load_ctx(t)

            eng.wait_ge(blank_ready, 1)
            early = 4
            for i in range(early):
                next_ctx(Tile(1 + i // 2, i % 2))
                for e in range(i * experts // early, (i + 1) * experts // early):
                    eng.dma_start(slot_rows[e], blank[:, :, :]).then_inc(blanked, 16)
            with eng.Fori(3, tiles // 2) as half:
                for ring in range(2):
                    next_ctx(Tile(half, ring))
            for e in range(2):
                eng.dma_start(w1_sb[:, e, :], w1[e]).then_inc(w1_loaded[e], 16)
                eng.dma_start(w2_sb[:, e, :, :], w2[e].rearrange("(f p) d -> p f d", p=P)).then_inc(w2_loaded[e], 16)
            eng.dma_start(b2_all[:, :, :], b2.rearrange("e d -> (e d)").partition_broadcast(P)).then_inc(b2_loaded, 16)

            for ring in range(2):
                eng.wait_ge(scattered[ring], 16 * TOP * (tiles // 2))
            for part, loaded in ((slice(0, turned_first), first_slots),
                                 (slice(turned_first, slot_tiles), xg_loaded[0])):
                eng.dma_start(xg[:, 0, part, :], slot_rows[0][:, part, 0:d_model]).then_inc(loaded, 16)
            eng.dma_start(xg[:, 1, :, :], slot_rows[1][:, :, 0:d_model]).then_inc(xg_loaded[1], 16)
            eng.dma_start(tails[:, :, :], slot_tails[:, :, d_model:row]).then_inc(tails_loaded, 16)

            def load_slots(e):
                eng.wait_ge(xg_turned, e.twice(-2))
                eng.dma_start(xg[:, e.ring, :, :], slot_rows[e.index][:, :, 0:d_model]).then_inc(xg_loaded[e.ring], 16)

            def load_expert(e, after):
                eng.wait_ge(up_done, f_tiles * (e.index - 1))
                eng.dma_start(w1_sb[:, e.ring, :], w1[e.index]).then_inc(w1_loaded[e.ring], 16)
                if after:
                    load_slots(after)
                eng.wait_ge(down_done, slot_tiles * (e.index - 1))
                eng.dma_start(w2_sb[:, e.ring, :, :],
                              w2[e.index].rearrange("(f p) d -> p f d", p=P)).then_inc(w2_loaded[e.ring], 16)

            eng.dma_start(out_tiles, x_res[:, :, :]).then_inc(residual_stored, 16)
            load_slots(Tile(1, 0))
            with eng.Fori(1, experts // 2 - 1) as half:
                load_expert(Tile(half, 0), Tile(half, 1))
                load_expert(Tile(half, 1), Tile(half + 1, 0))
            load_expert(Tile(experts // 2 - 1, 0), Tile(experts // 2 - 1, 1))
            load_expert(Tile(experts // 2 - 1, 1), None)

            for ring in range(2):
                eng.wait_ge(y_stored[ring], 16 * slot_tiles * (experts // 2))

        @block.gpsimd
        def _(eng):
            eng.memset(ident[:, :], 0.0).then_inc(pool_const, 1)
            eng.memset(ones[:, :], 1.0).then_inc(pool_const, 1)
            eng.memset(minus_half[:, :], -0.5).then_inc(pool_const, 1)
            eng.memset(eps[:, :], LN_EPS)
            eng.memset(band[:, :], 1.0).then_inc(pool_const, 1)
            eng.wait_ge(pool_const, 4)
            eng.affine_select(out=ident[:, :], in_=ident[:, :], compare_op=ALU.not_equal, fill=1.0, base=0,
                              pattern=[[-1, P]], channel_multiplier=1).then_inc(pool_const, 1)
            eng.affine_select(out=band[:, :], in_=band[:, :], compare_op=ALU.is_ge, fill=0.0, base=0,
                              pattern=[[-d_head, HEADS]], channel_multiplier=1).then_inc(pool_const, 1)
            eng.wait_ge(pool_const, 6)
            eng.affine_select(out=band[:, :], in_=band[:, :], compare_op=ALU.is_ge, fill=0.0, base=d_head - 1,
                              pattern=[[d_head, HEADS]], channel_multiplier=-1).then_inc(pool_const, 1)
            eng.affine_select(out=tri[:, :], in_=ones[:, :], compare_op=ALU.is_ge, fill=0.0, base=0,
                              pattern=[[1, P]], channel_multiplier=-1).then_inc(pool_const, 1)
            eng.iota(expert_ids[:, :], pattern=[[1, experts]], base=0, channel_multiplier=0,
                     allow_small_or_imprecise_dtypes=True).then_inc(pool_const, 1)
            eng.iota(slot_base[:, :, :], pattern=[[capacity, TOP], [per_expert, experts]], base=-1,
                     channel_multiplier=0, allow_small_or_imprecise_dtypes=True).then_inc(pool_const, 1)
            eng.iota(dest_ids[:, :, :], pattern=[[P, tiles], [0, TOP]], base=0, channel_multiplier=1,
                     allow_small_or_imprecise_dtypes=True).then_inc(pool_const, 1)
            eng.memset(over[:, :, :], OUT_OF_BOUNDS).then_inc(pool_const, 1)
            eng.memset(taken[:, 0, :, :], 0.0).then_inc(s["taken"], 1)
            eng.memset(blank[:, :, 0:dest_at], 0.0)
            eng.memset(blank[:, :, weight_at:row], 0.0)
            eng.iota(blank[:, :, dest_at:dest_at + TOP], pattern=[[P, slot_tiles], [0, TOP]], base=tokens,
                     channel_multiplier=1, allow_small_or_imprecise_dtypes=True).then_inc(blank_ready, 1)

            x_parts = [slice(tiles * i // 2, tiles * (i + 1) // 2) for i in range(2)]

            def step(half, ring, known):
                at = (half, ring, known)
                t = stage(at, 6)
                if t:
                    if known == 6:
                        eng.wait_ge(blanked, 16 * experts)
                    eng.wait_ge(s["slot_at"], t.plus(1))
                    eng.wait_ge(s["dests"], t.plus(1))
                    eng.sem_inc(pool_waited, 1)
                    for k in range(TOP):
                        eng.indirect_dma_start(
                            out=slots[:, :], out_offset=bass.IndirectOffsetOnAxis(ap=slot_at[:, t.ring, k:k + 1], axis=0),
                            in_=rows[:, t.ring, :], in_offset=None, bounds_check=n_slots - 1,
                            oob_is_err=False).then_inc(scattered[t.ring], 16)
                t = stage(at, 5)
                if t:
                    if reused(t):
                        eng.wait_ge(scattered[t.ring], t.earlier(16 * TOP))
                    eng.tensor_copy(rows[:, t.ring, dest_at:dest_at + TOP],
                                    dest_ids[:, t.index, :]).then_inc(s["dests"], 1)

                def mask_queries():
                    t = stage(at, 1)
                    if t:
                        eng.wait_ge(s["q_copied"], t.plus(1))
                        if known == 1:
                            eng.wait_ge(pool_mask, 1)
                        for b in range(2):
                            last = eng.tensor_tensor(
                                Qm[:, t.ring, b, :, :],
                                qT[:, t.ring, b * seq:(b + 1) * seq].unsqueeze(1).broadcast_to([P, STRIPS, seq]),
                                head_mask[:, :].unsqueeze(2).broadcast_to([P, STRIPS, seq]), ALU.mult)
                        last.then_inc(s["q_masked"], 1)

                def inverse_deviations():
                    first, second = stage(at, 0), stage(at, 4)
                    if first or second:
                        t = first or second
                        if second:
                            eng.wait_ge(s["mv2"], second.plus(1))
                        else:
                            eng.wait_ge(s["mv1"], first.plus(1))
                        now = Tile(half, ring)
                        if known == 0:
                            eng.wait_ge(dve_const, 3)
                        eng.tensor_tensor(var[:, :], mv[:, t.ring, :, 1], eps[:, :], ALU.add).then_inc(s["var"], 1)
                        eng.wait_ge(s["var"], now.plus(1))
                        eng.tensor_tensor(rstd[:, t.ring, :], var[:, :], minus_half[:, :],
                                          ALU.pow).then_inc(s["rstd"], 1)

                if filling(known):
                    inverse_deviations()
                    mask_queries()
                else:
                    mask_queries()
                t = stage(at, 5)
                if t:
                    eng.wait_ge(s["onehot"], t.plus(1))
                    eng.wait_ge(s["taken"], t.plus(1))
                    eng.tensor_tensor(taken[:, 1 - t.ring, :, :], taken[:, t.ring, :, :], onehot[:, t.ring, :, :],
                                      ALU.add).then_inc(s["taken"], 1)
                if not filling(known):
                    inverse_deviations()
                if known in (2, 3):
                    if known == 2:
                        eng.wait_ge(gated_bo, 1)
                        for piece in x_loaded:
                            eng.wait_ge(piece, 16)
                    part = x_parts[known - 2]
                    eng.tensor_tensor(x_res[:, part, :], x_sb[:, part, :],
                                      bo_all[:, :].unsqueeze(1).broadcast_to([P, part.stop - part.start, d_model]),
                                      ALU.add).then_inc(s["x_bo"], 1)

            run_steps(eng, step)

            def send_rows(e):
                eng.wait_ge(slot_fields, e.index + 1)
                eng.wait_ge(residual_stored, 16)
                if after_first(e):
                    last = 1 - e.ring
                    eng.wait_ge(y_stored[last], 16 * slot_tiles * (e.half + e.ring))
                for c in range(slot_tiles):
                    eng.wait_ge(y_ready, slot_tiles * e.index + c + 1)
                    eng.sem_inc(pool_waited, 1)
                    eng.indirect_dma_start(
                        out=out_rows, out_offset=bass.IndirectOffsetOnAxis(ap=slot_dest[:, e.ring, c:c + 1], axis=0),
                        in_=y_sb[:, e.ring, c, :], in_offset=None, bounds_check=tokens - 1,
                        oob_is_err=False, compute_op=ALU.add).then_inc(y_stored[e.ring], 16)

            send_rows(Tile(0, 0))
            send_rows(Tile(0, 1))
            with eng.Fori(1, experts // 2) as half:
                for ring in range(2):
                    send_rows(Tile(half, ring))

        @block.scalar
        def _(eng):
            eng.wait_ge(attn_weights, 32)
            eng.activation(bq_scaled[:, :], wq_sb[:, d_model:d_model + 1], ACT.Copy, scale=scale).then_inc(bq_ready, 1)
            eng.wait_ge(bq_ready, 1)

            def step(half, ring, known):
                at = (half, ring, known)
                x_tile, o_tile, x2_tile = stage(at, 1), stage(at, 4), stage(at, 5)

                def copy_operands():
                    if x_tile or o_tile or x2_tile:
                        eng.wait_ge(s["turned"], Tile(half, ring).index)
                        begin = X_AT if x_tile else O_AT if o_tile else X2_AT
                        end = X2_AT + 1 if x2_tile else X2_AT if o_tile else O_AT
                        last = eng.activation(turned[:, ring, begin:end, :], act_bank[:, begin * P:end * P], ACT.Copy)
                        if x_tile:
                            if known == 1:
                                eng.wait_ge(dve_const, 3)
                            last = eng.activation(cT[0:d_ctx, ring, :], o_bank[0:d_ctx, 3 * P:4 * P], ACT.Copy)
                        last.then_inc(s["turns_copied"], 1)

                def exponentials():
                    t = stage(at, 3)
                    if t:
                        for h in range(2):
                            eng.wait_ge(s["probs_turned"], t.twice(h + 1))
                            eng.activation(probsT[:, t.ring, 4 * h:4 * h + 4, :],
                                           turn_bank[h][:, :], ACT.Exp).then_inc(s["probsT"], 1)

                def copy_projections():
                    t = stage(at, 1)
                    if t:
                        eng.wait_ge(s["qkv"], t.plus(1))
                        eng.activation(qT[:, t.ring, :], qkv_bank[:, 0:P], ACT.Identity, bias=bq_scaled[:, 0:1],
                                       scale=scale).then_inc(s["q_copied"], 1)
                        for j in range(STRIPS):
                            r = slice(32 * j, 32 * j + 32)
                            last = eng.activation(Km[r, t.ring, :, j, :],
                                                  qkv_bank[r, P:2 * P].rearrange("p (b k) -> p b k", b=2), ACT.Copy)
                        last.then_inc(s["k_copied"], 1)

                if filling(known):
                    copy_operands()
                    copy_projections()
                    exponentials()
                elif draining(known):
                    exponentials()
                    copy_operands()
                else:
                    copy_operands()
                    exponentials()
                    copy_projections()
                t = stage(at, 5)
                if t:
                    eng.wait_ge(s["minus_top"], t.plus(1))
                    eng.activation(top_exp[:, t.ring, :], top8[:, t.ring, 0:TOP], ACT.Exp,
                                   bias=minus_top[:, t.ring:t.ring + 1],
                                   accum_out=top_sum[:, t.ring:t.ring + 1]).then_inc(s["top_exp"], 1)
                if known == 2:
                    eng.wait_ge(gates_loaded, 16)
                    eng.activation(gates[:, :], gates_in[:, :], ACT.Tanh).then_inc(gate_ready, 1)
                    eng.wait_ge(bias_turned, 1)
                    eng.activation(bias_cols[:, :], out_bank[:, 0:experts * f_tiles], ACT.Copy).then_inc(bias_ready, 1)
                    eng.wait_ge(bias_ready, 1)
                t = stage(at, 1)
                if t:
                    if reused(t):
                        eng.wait_ge(s["pv"], t.plus(-1))
                    for b in range(2):
                        own = slice(64 * b, 64 * b + 64)
                        last = eng.activation(Vbd[own, t.ring, :, b, 0:2 * d_head],
                                              qkv_bank[own, 2 * P:3 * P].rearrange("p (h m) -> p h m", m=2 * d_head),
                                              ACT.Copy)
                    last.then_inc(s["v_copied"], 1)

            run_steps(eng, step)

            def gelus(e):
                for f in range(f_tiles):
                    eng.wait_ge(up_done, e.index * f_tiles + f + 1)
                    if reused(e):
                        eng.wait_ge(down_done, slot_tiles * (e.index - 1))
                    for h in range(2):
                        last = eng.activation(
                            hT[:, e.ring, f, h * capacity:(h + 1) * capacity], bank[2 * (f % 2) + h][:, 0:capacity],
                            ACT.Gelu, bias=bias_cols[:, bass.ds(e.index * f_tiles + f, 1)])
                    last.then_inc(gelu_done, 1)

            gelus(Tile(0, 0))
            gelus(Tile(0, 1))
            with eng.Fori(1, experts // 2) as half:
                for ring in range(2):
                    gelus(Tile(half, ring))

        @block.vector
        def _(eng):
            eng.memset(warm[:, :], 0.0).then_inc(warm_ready, 1)
            eng.memset(Km[:, :, :, :, :], 0.0)
            eng.memset(Vbd[:, :, :, :, 0:2 * d_head], 0.0).then_inc(dve_const, 1)
            for b in range(2):
                own = slice(64 * b, 64 * b + 64)
                for c in range(2):
                    last = eng.memset(Vbd[own, :, :, c, 2 * d_head:v_cols], 1.0 if b == c else 0.0)
            last.then_inc(dve_const, 1)
            eng.memset(cT[d_ctx:d_ctx + 1, :, :], 1.0)
            eng.memset(mv[:, :, :, :], 1.0).then_inc(dve_const, 1)
            eng.wait_ge(pool_const, 12)
            eng.tensor_reduce(head_mask[:, :], band[:, :].rearrange("p (s h) -> p h s", h=STRIPS), AX.X,
                              ALU.add)
            eng.tensor_reduce(parity[:, :], band[:, :].rearrange("p (h j) -> p j h", j=2), AX.X,
                              ALU.add).then_inc(pool_mask, 1)
            eng.wait_ge(dve_const, 3)

            def take_stats(t, source, stats, name):
                eng.bn_stats(stats[:, :], source).then_inc(s[name], 1)

            def aggregate(t, stats, which, stats_name, done):
                eng.wait_ge(s[stats_name], t.plus(1))
                eng.sem_inc(dve_waited, 1)
                eng.bn_aggr(mv[:, t.ring, which, :], stats[:, :]).then_inc(s[done], 1)

            def normalise(t, source, which, to, done):
                eng.tensor_scalar(to, source, mv[:, t.ring, which, 0:1], rstd[:, t.ring, which:which + 1],
                                  ALU.subtract, ALU.mult).then_inc(s[done], 1)

            def find_maxima(t, b):
                eng.wait_ge(s["scores"], t.twice(b + 1))
                scores = score_bank[b][:, :].rearrange("p (g s k) -> p g s k", g=2, k=seq)
                eng.tensor_reduce(row_max[:, b, :, :], scores, AX.X, ALU.max).then_inc(s["maxima"], 1)

            def shift_scores(t, b):
                eng.wait_ge(s["maxima"], t.twice(b + 1))
                scores = score_bank[b][:, :].rearrange("p (g s k) -> p g s k", g=2, k=seq)
                eng.tensor_tensor(probs[:, t.ring, :, b, :].rearrange("p (s g) k -> p g s k", g=2), scores,
                                  row_max[:, b, :, :].unsqueeze(3).broadcast_to([P, 2, STRIPS, seq]),
                                  ALU.subtract).then_inc(s["shifted"], 1)

            def step(half, ring, known):
                at = (half, ring, known)
                stats_tile, x_tile, score_tile = stage(at, 0), stage(at, 1), stage(at, 2)
                o_tile, route_tile = stage(at, 4), stage(at, 5)
                o = o_bank[:, 0:PAIRS * 2 * v_cols].rearrange("p (h b m) -> p h b m", b=2, m=v_cols)

                if o_tile:
                    t = o_tile
                    eng.wait_ge(s["pv"], t.plus(1))
                    eng.reciprocal(denom[:, :, :], o[:, :, :, 2 * d_head]).then_inc(s["recips"], 1)
                if route_tile:
                    t = route_tile
                    eng.wait_ge(s["rstd"], t.plus(5))
                    if reused(t):
                        eng.wait_ge(scattered[t.ring], t.earlier(16 * TOP))
                    normalise(t, x_res[:, t.index, :], 1, rows[:, t.ring, 0:d_model], "xn2")
                if x_tile:
                    t = x_tile
                    eng.wait_ge(s["rstd"], t.plus(1))
                    if after_first(t) and not o_tile:
                        eng.wait_ge(s["turned"], t.index)
                    normalise(t, x_sb[:, t.index, :], 0, xn1[:, :], "xn1")
                if o_tile:
                    t = o_tile
                    eng.wait_ge(s["recips"], t.plus(1))
                    eng.tensor_tensor(o_norm[:, :, :, :].rearrange("p b h m -> p h b m"), o[:, :, :, 0:2 * d_head],
                                      denom[:, :, :].unsqueeze(3).broadcast_to([P, PAIRS, 2, 2 * d_head]),
                                      ALU.mult).then_inc(s["o_norm"], 1)
                def begin_first_norm():
                    if stats_tile:
                        t = stats_tile
                        for (first, _), piece_loaded in zip(x_pieces, x_loaded):
                            if known == min(first, PEELED_STEPS - 1):
                                eng.wait_ge(piece_loaded, 16)
                        take_stats(t, x_sb[:, t.index, :], stats1, "stats1")

                def end_first_norm():
                    if stats_tile:
                        aggregate(stats_tile, stats1, 0, "stats1", "mv1")

                if filling(known):
                    begin_first_norm()
                    end_first_norm()
                if score_tile:
                    for b in range(2):
                        find_maxima(score_tile, b)
                    for b in range(2):
                        shift_scores(score_tile, b)
                if not filling(known):
                    begin_first_norm()
                if known == 2:
                    eng.wait_ge(gate_ready, 1)
                    eng.wait_ge(small_weights, 16 * 3)
                    eng.tensor_scalar(bo_all[:, :], bo_all[:, :], gates[:, 0:1], None, ALU.mult).then_inc(gated_bo, 1)
                    eng.wait_ge(pool_mask, 1)
                    for j in range(2):
                        last = eng.tensor_scalar(wo_own[:, j, :], wo_sb[:, :], parity[:, j:j + 1], None, ALU.mult)
                    last.then_inc(wo_masked, 1)
                if not filling(known):
                    end_first_norm()
                logits = out_bank[:, P:P + experts]
                if route_tile:
                    t = route_tile
                    eng.wait_ge(s["logits"], t.plus(1))
                    eng.sem_inc(dve_waited, 1)
                    eng.max(top8[:, t.ring, :], logits).then_inc(s["top8"], 1)
                if o_tile:
                    t = o_tile
                    if not route_tile:
                        eng.wait_ge(s["projected"], t.plus(1))
                    if known == 4:
                        eng.wait_ge(s["x_bo"], 2)
                    eng.scalar_tensor_tensor(out=x_res[:, t.index, :], in0=out_bank[:, 0:P], scalar=gates[:, 0:1],
                                             in1=x_res[:, t.index, :], op0=ALU.mult, op1=ALU.add).then_inc(s["x1"], 1)
                if route_tile:
                    t = route_tile
                    eng.wait_ge(s["top8"], t.plus(1))
                    eng.sem_inc(dve_waited, 1)
                    eng.max_index(top8_at[:, :], top8[:, t.ring, :], logits).then_inc(s["top8_at"], 1)
                    eng.tensor_scalar(minus_top[:, t.ring:t.ring + 1], top8[:, t.ring, 0:1], -1.0, None,
                                      ALU.mult).then_inc(s["minus_top"], 1)
                if o_tile:
                    t = o_tile
                    eng.wait_ge(s["x1"], t.plus(1))
                    eng.sem_inc(dve_waited, 1)
                    take_stats(t, x_res[:, t.index, :], stats2, "stats2")
                if route_tile:
                    t = route_tile
                    eng.wait_ge(s["top8_at"], t.plus(1))
                    eng.tensor_tensor(onehot[:, t.ring, :, :],
                                      expert_ids[:, :].unsqueeze(1).broadcast_to([P, TOP, experts]),
                                      top8_at[:, 0:TOP].unsqueeze(2).broadcast_to([P, TOP, experts]),
                                      ALU.is_equal).then_inc(s["onehot"], 1)
                if o_tile:
                    aggregate(o_tile, stats2, 1, "stats2", "mv2")
                if route_tile:
                    t = route_tile
                    rank = out_bank[:, 144:144 + TOP * experts].rearrange("p (k e) -> p k e", k=TOP)
                    eng.wait_ge(s["ranks"], t.plus(1))
                    eng.scalar_tensor_tensor(out=over_cap[:, :, :], in0=rank, scalar=float(capacity),
                                             in1=over[:, :, :], op0=ALU.is_gt, op1=ALU.mult)
                    eng.tensor_tensor(based[:, :, :], rank, slot_base[:, :, :], ALU.add).then_inc(s["capped"], 1)
                    eng.wait_ge(s["top_exp"], t.plus(1))
                    eng.reciprocal(top_inv[:, :], top_sum[:, t.ring:t.ring + 1]).then_inc(s["top_inv"], 1)
                    eng.wait_ge(s["capped"], t.plus(1))
                    eng.tensor_tensor(at_any[:, :, :], over_cap[:, :, :], based[:, :, :],
                                      ALU.add).then_inc(s["at_any"], 1)
                    eng.wait_ge(s["top_inv"], t.plus(1))
                    eng.tensor_scalar(rows[:, t.ring, weight_at:weight_at + TOP], top_exp[:, t.ring, :],
                                      top_inv[:, 0:1], gates[:, 1:2], ALU.mult, ALU.mult).then_inc(s["weights"], 1)
                    eng.wait_ge(s["at_any"], t.plus(1))
                    eng.tensor_tensor(at_own[:, :, :], at_any[:, :, :], onehot[:, t.ring, :, :],
                                      ALU.mult).then_inc(s["at_own"], 1)
                    eng.wait_ge(s["at_own"], t.plus(1))
                    with nc.allow_low_precision(reason="the sum of one whole number and zeros, exact in int32"):
                        eng.tensor_reduce(slot_at[:, t.ring, :], at_own[:, :, :], AX.X,
                                          ALU.add).then_inc(s["slot_at"], 1)

            run_steps(eng, step)

            def turn_in(e):
                split = turned_first * P
                eng.wait_ge(xg_turned, e.twice(1))
                if reused(e):
                    eng.wait_ge(up_done, f_tiles * (e.index - 1))
                eng.tensor_copy(xgT[:, e.ring, 0:split], bank[6][:, 0:split]).then_inc(xgT_ready, 1)
                eng.wait_ge(xg_turned, e.twice(2))
                eng.tensor_copy(xgT[:, e.ring, split:per_expert], bank[7][:, 0:per_expert - split]).then_inc(xgT_ready, 1)

            def pick_tails():
                eng.wait_ge(tails_loaded, 16)
                fields = tails[:, :, :].rearrange("p (e c) w -> p e c w", e=experts)
                for to, at in ((all_w, TOP), (all_dest, 0)):
                    eng.tensor_copy(to[:, :, 0:first_tiles], fields[:, :, 0:first_tiles, at])
                    for part, k in ((slice(0, first_rest), 0), (slice(first_rest, P), 1)):
                        eng.tensor_copy(to[part, :, first_tiles], fields[part, :, first_tiles, at + k])
                    last = eng.tensor_copy(to[:, :, first_tiles + 1:slot_tiles],
                                           fields[:, :, first_tiles + 1:slot_tiles, at + 1])
                last.then_inc(tails_picked, 1)
                eng.wait_ge(tails_picked, 1)

            def take_fields(e):
                if reused(e):
                    eng.wait_ge(y_stored[e.ring], 16 * slot_tiles * e.half)
                    eng.wait_ge(y_ready, slot_tiles * (e.index - 1))
                eng.tensor_copy(slot_w[:, e.ring, :].unsqueeze(1), all_w[:, bass.ds(e.index, 1), :])
                eng.tensor_copy(slot_dest[:, e.ring, :].unsqueeze(1),
                                all_dest[:, bass.ds(e.index, 1), :]).then_inc(slot_fields, 1)

            def turn_out(e):
                eng.wait_ge(slot_fields, e.index + 1)
                if reused(e):
                    eng.wait_ge(y_stored[e.ring], 16 * slot_tiles * e.half)
                for c in range(slot_tiles):
                    n = slot_tiles * e.index + c
                    part = (e.ring + c) % 2
                    eng.wait_ge(down_done, n + 1)
                    if not isinstance(n, int) or n >= 2:
                        eng.wait_ge(y_ready, n - 1)
                    eng.tensor_tensor(y_plus[:, part, :].unsqueeze(1), bank[4 + part][:, 0:d_model].unsqueeze(1),
                                      b2_all[:, bass.ds(e.index, 1), :], ALU.add).then_inc(y_biased, 1)
                    eng.wait_ge(y_biased, n + 1)
                    eng.tensor_scalar(y_sb[:, e.ring, c, :], y_plus[:, part, :], slot_w[:, e.ring, c:c + 1], None,
                                      ALU.mult).then_inc(y_ready, 1)

            turn_in(Tile(0, 0))
            turn_in(Tile(0, 1))
            pick_tails()
            take_fields(Tile(0, 0))
            turn_in(Tile(1, 0))
            eng.wait_ge(b2_loaded, 16)
            turn_out(Tile(0, 0))
            take_fields(Tile(0, 1))
            with eng.Fori(1, experts // 2 - 1) as half:
                turn_in(Tile(half, 1))
                turn_out(Tile(half - 1, 1))
                take_fields(Tile(half, 0))
                turn_in(Tile(half + 1, 0))
                turn_out(Tile(half, 0))
                take_fields(Tile(half, 1))
            end = experts // 2 - 1
            turn_in(Tile(end, 1))
            turn_out(Tile(end - 1, 1))
            take_fields(Tile(end, 0))
            turn_out(Tile(end, 0))
            take_fields(Tile(end, 1))
            turn_out(Tile(end, 1))

        @block.tensor
        def _(eng):
            def keep_warm(products, unused=bank[0]):
                for i in range(products):
                    eng.matmul(unused[:, :], warm[:, 0:P], warm[:, :], start=True, stop=True)

            def step(half, ring, known):
                at = (half, ring, known)
                x_tile, o_tile, route_tile = stage(at, 1), stage(at, 4), stage(at, 5)

                def score():
                    t = stage(at, 2)
                    if t:
                        eng.wait_ge(s["q_masked"], t.plus(1))
                        eng.wait_ge(s["k_copied"], t.plus(1))
                        for b in range(2):
                            if after_first(t):
                                eng.wait_ge(s["shifted"], t.twice(b - 1))
                            for g in range(2):
                                mm = eng.matmul(score_bank[b][:, 256 * g:256 * g + 256],
                                                Qm[:, t.ring, b, 2 * g:2 * g + 2, :].rearrange("p j q -> p (j q)"),
                                                Km[:, t.ring, b, :, :].rearrange("p s k -> p (s k)"),
                                                start=True, stop=True)
                            mm.then_inc(s["scores"], 1)

                def turn_operands():
                    if route_tile:
                        t = route_tile
                        eng.wait_ge(s["xn2"], t.plus(1))
                        mm = eng.transpose(act_bank[:, X2_AT * P:(X2_AT + 1) * P], rows[:, t.ring, 0:d_model], ident[:, :])
                    if x_tile:
                        t = x_tile
                        eng.wait_ge(ctx_loaded[t.ring], t.earlier(16) + 16)
                        eng.wait_ge(s["xn1"], t.plus(1))
                        eng.transpose(act_bank[:, X_AT * P:(X_AT + 1) * P], xn1[:, :], ident[:, :])
                    if o_tile:
                        t = o_tile
                        eng.wait_ge(s["o_norm"], t.plus(1))
                        for b in range(2):
                            mm = eng.transpose(
                                act_bank[:, O_AT * P:(O_AT + 2) * P].rearrange("p (j b q) -> p j b q", j=2, b=2)[:, :, b, :],
                                o_norm[:, b, :, :].rearrange("p h m -> p (h m)"), ident[:, :])
                    if x_tile:
                        t = x_tile
                        mm = eng.transpose(o_bank[0:d_ctx, 3 * P:4 * P], ctx_sb[:, t.ring, :], ident[:, :])
                    if x_tile or o_tile or route_tile:
                        mm.then_inc(s["turned"], 1)

                def turn_probs():
                    t = stage(at, 3)
                    if t:
                        if not stage(at, 2):
                            eng.wait_ge(s["shifted"], t.twice(2))
                        for h in range(2):
                            for i in range(4):
                                p = 4 * h + i
                                mm = eng.transpose(turn_bank[h][:, i * P:(i + 1) * P],
                                                   probs[:, t.ring, p, :, :].rearrange("p b k -> p (b k)"), ident[:, :])
                            mm.then_inc(s["probs_turned"], 1)

                def project():
                    if x_tile or o_tile or route_tile:
                        eng.wait_ge(s["turns_copied"], Tile(half, ring).index)
                    if x_tile:
                        t = x_tile
                        if known == 1:
                            eng.wait_ge(attn_weights, 32)
                        if after_first(t):
                            eng.wait_ge(s["v_copied"], t.index)
                        eng.matmul(qkv_bank[:, 0:P], wq_sb[:, 0:d_model], turned[:, ring, X_AT, :], start=True, stop=True)
                        eng.matmul(qkv_bank[:, P:2 * P], wkv_sb[:, 0:d_model], cT[:, ring, :], start=True, stop=True)
                        eng.matmul(qkv_bank[:, 2 * P:3 * P], cT[:, ring, :], wkv_sb[:, d_model:2 * d_model], start=True,
                                   stop=True).then_inc(s["qkv"], 1)

                if filling(known):
                    turn_operands()
                    if x_tile:
                        keep_warm(WARM_COPY, turn_bank[0])
                    project()
                    score()
                    turn_probs()
                elif draining(known):
                    turn_probs()
                    turn_operands()
                    keep_warm(WARM_COPY)
                    project()
                else:
                    score()
                    turn_operands()
                    turn_probs()
                    project()
                if known == 2:
                    eng.wait_ge(b1_loaded, 16)
                    n_b1 = experts * f_tiles
                    eng.transpose(out_bank[:, 0:n_b1], bias_rows[:, :], ident[0:n_b1, 0:n_b1]).then_inc(bias_turned, 1)
                if o_tile or route_tile:
                    if known == 5:
                        eng.wait_ge(s["x1"], 1)
                    if known is None or known >= 6:
                        eng.wait_ge(s["capped"], Tile(half, ring).plus(-5))
                if o_tile:
                    if known == 4:
                        eng.wait_ge(wo_masked, 1)
                        eng.wait_ge(bias_ready, 1)
                    for j in range(2):
                        mm = eng.matmul(out_bank[:, 0:P], turned[:, ring, O_AT + j, :], wo_own[:, j, :],
                                        start=(j == 0), stop=(j == 1))
                    mm.then_inc(s["projected"], 1)
                if route_tile:
                    if known == 5:
                        eng.wait_ge(small_weights, 16 * 3)
                    eng.matmul(out_bank[:, P:P + experts], turned[:, ring, X2_AT, :], wr_sb[:, :], start=True,
                               stop=True).then_inc(s["logits"], 1)
                pv_tile = stage(at, 3)

                def weigh_values(pairs):
                    t = pv_tile
                    for p in pairs:
                        if p % 4 == 0:
                            eng.wait_ge(s["probsT"], t.twice(p // 4 + 1))
                        mm = eng.matmul(o_bank[:, p * 2 * v_cols:(p + 1) * 2 * v_cols], probsT[:, t.ring, p, :],
                                        Vbd[:, t.ring, p].rearrange("p b m -> p (b m)"), start=True, stop=True)
                    return mm

                if pv_tile:
                    if known is not None and known > tiles + 1:
                        eng.wait_ge(s["v_copied"], pv_tile.plus(1))
                    weigh_values(range(PAIRS - LAST_PAIRS))
                if draining(known) and not pv_tile:
                    keep_warm(WARM_CHOICE)
                if route_tile:
                    t = route_tile
                    eng.wait_ge(s["onehot"], t.plus(1))
                    eng.wait_ge(s["taken"], t.plus(1))
                    eng.matmul(out_bank[:, 144:144 + TOP * experts], tri[:, :],
                               onehot[:, t.ring, :, :].rearrange("p k e -> p (k e)"), start=True, stop=False)
                    eng.matmul(out_bank[:, 144:144 + TOP * experts], ones[:, :],
                               taken[:, t.ring, :, :].rearrange("p k e -> p (k e)"), start=False,
                               stop=True).then_inc(s["ranks"], 1)
                if pv_tile:
                    weigh_values(range(PAIRS - LAST_PAIRS, PAIRS)).then_inc(s["pv"], 1)
                if draining(known):
                    keep_warm(WARM_STEP)
                if filling(known) and x_tile:
                    keep_warm(WARM_STEP, turn_bank[0])

            eng.wait_ge(warm_ready, 1)
            keep_warm(WARM_START)
            eng.wait_ge(pool_const, 12)
            run_steps(eng, step)

            def turn_rows(e):
                if after_first(e):
                    eng.wait_ge(xg_loaded[e.ring], 16 * (e.half + 1))
                    eng.wait_ge(xgT_ready, e.twice(0))
                else:
                    eng.wait_ge(first_slots, 16)
                for c in range(turned_first):
                    mm = eng.transpose(bank[6][:, c * P:(c + 1) * P], xg[:, e.ring, c, 0:d_model], ident[:, :])
                mm.then_inc(xg_turned, 1)
                if not after_first(e):
                    eng.wait_ge(xg_loaded[e.ring], 16)
                for c in range(slot_tiles - turned_first):
                    mm = eng.transpose(bank[7][:, c * P:(c + 1) * P], xg[:, e.ring, turned_first + c, 0:d_model],
                                       ident[:, :])
                mm.then_inc(xg_turned, 1)

            def up(e, f):
                if f == 0:
                    eng.wait_ge(w1_loaded[e.ring], 16 * (e.half + 1))
                if f >= 2 or after_first(e):
                    eng.wait_ge(gelu_done, e.index * f_tiles + f - 1)
                for h in range(2):
                    if f == 0:
                        eng.wait_ge(xgT_ready, e.twice(h + 1))
                    mm = eng.matmul(bank[2 * (f % 2) + h][:, 0:capacity], w1_sb[:, e.ring, f * P:(f + 1) * P],
                                    xgT[:, e.ring, h * capacity:(h + 1) * capacity], start=True, stop=True)
                mm.then_inc(up_done, 1)

            def down(e, c):
                if c == 0:
                    eng.wait_ge(gelu_done, (e.index + 1) * f_tiles)
                    eng.wait_ge(w2_loaded[e.ring], 16 * (e.half + 1))
                n = slot_tiles * e.index + c
                if not isinstance(n, int) or n >= 2:
                    eng.wait_ge(y_biased, n - 1)
                for f in range(f_tiles):
                    mm = eng.matmul(bank[4 + (e.ring + c) % 2][:, 0:d_model],
                                    hT[:, e.ring, f, c * P:(c + 1) * P], w2_sb[:, e.ring, f, :],
                                    start=(f == 0), stop=(f == f_tiles - 1))
                mm.then_inc(down_done, 1)

            def expert(e, before, after, at_once=1):
                for f in range(f_tiles):
                    up(e, f)
                    if f == 0 and after:
                        turn_rows(after)
                    if before:
                        end = slot_tiles if f == f_tiles - 1 else (f + 1) * at_once
                        for c in range(f * at_once, min(end, slot_tiles)):
                            down(before, c)

            eng.wait_ge(s["slot_at"], tiles)
            keep_warm(WARM_EXPERTS)

            turn_rows(Tile(0, 0))
            expert(Tile(0, 0), None, Tile(0, 1))
            expert(Tile(0, 1), Tile(0, 0), Tile(1, 0))
            with eng.Fori(1, experts // 2 - 1) as half:
                expert(Tile(half, 0), Tile(half - 1, 1), Tile(half, 1))
                expert(Tile(half, 1), Tile(half, 0), Tile(half + 1, 0))
            end = experts // 2 - 1
            expert(Tile(end, 0), Tile(end - 1, 1), Tile(end, 1))
            expert(Tile(end, 1), Tile(end, 0), None, at_once=2)
            for c in range(slot_tiles):
                down(Tile(end, 1), c)


def kernel(**inputs):
    import numpy as _np
    import concourse.bacc as _bacc
    from concourse import mybir as _mybir
    from concourse.bass_utils import run_bass_kernel_spmd as _run

    nc = _bacc.Bacc("TRN2", target_bir_lowering=False, num_devices=1)
    arrays, args = {}, []
    np_in = {name: _np.asarray(a) for name, a in inputs.items()}
    laid_out = [
        ("x", np_in["x"]),
        ("ctx_512", np_in["ctx_512"]),
        ("gates", _np.concatenate([np_in["g_xattn"], np_in["g_ffn"]])),
        ("Wq_bq", _np.concatenate([np_in["L0_xattn_Wq"], np_in["L0_xattn_bq"][:, None]], axis=1)),
        ("Wkv_bkv", _np.concatenate([
            _np.concatenate([np_in["L0_xattn_Wk"], np_in["L0_xattn_Wv"]], axis=1),
            _np.concatenate([np_in["L0_xattn_bk"], np_in["L0_xattn_bv"]])[None, :]], axis=0)),
    ] + [(name, np_in[name]) for name in ("L0_xattn_Wo", "L0_xattn_bo", "L0_ffn_Wr", "L0_ffn_W1", "L0_ffn_b1",
                                          "L0_ffn_W2", "L0_ffn_b2")]
    for name, a in laid_out:
        a = _np.ascontiguousarray(a)
        arrays[f"in_{name}_dram"] = a
        args.append(nc.dram_tensor(f"in_{name}_dram", a.shape, _mybir.dt.from_np(a.dtype), kind="ExternalInput").ap())
    shape = tuple(inputs["x"].shape)
    tokens, width = shape[0] * shape[1], shape[2]
    experts = inputs["L0_ffn_W1"].shape[0]
    capacity = max(1, int(tokens * CAPACITY_FACTOR / experts))
    out = nc.dram_tensor("out_0_dram", shape, F32, kind="ExternalOutput").ap()
    slots = nc.dram_tensor("slots", (experts * TOP * capacity, width + 2 * TOP), F32, kind="Internal").ap()
    flamingo_block(nc, *args, out, slots)
    r = _run(nc, [arrays], core_ids=[0])
    return r.results[0]["out_0_dram"]
```
